# Optimizing a Trainium2 kernel written in Bass

```python
import numpy as np
import jax
import jax.numpy as jnp

def _softmax(x, axis=-1):
    return jax.nn.softmax(x, axis=axis)

def _gelu(x):
    return jax.nn.gelu(x, approximate=True)

def _silu(x):
    return jax.nn.silu(x)

def _sigmoid(x):
    return jax.nn.sigmoid(x)

def _layernorm(x, axis=-1, eps=1e-05):
    m = jnp.mean(x, axis=axis, keepdims=True)
    v = jnp.var(x, axis=axis, keepdims=True)
    return (x - m) / jnp.sqrt(v + eps)

def _scatter_add(tgt, idx, src, axis=0):
    return tgt.at[idx].add(src)

def _segment_sum(src, seg, n):
    return jax.ops.segment_sum(src, seg, n)
kernel_name = 'mk_seq_postln_d1_jaxref_r8_c46488'

def setup_inputs(seed: int=0):
    np.random.seed(seed)
    _w = jnp.asarray

    def _L0_attn_setup():
        import jax, jax.numpy as jnp
        import numpy as np
        B, L, D_MODEL, D_STATE, D_HIDDEN = (4, 512, 128, 32, 512)
        RMIN, RMAX, MAX_PHASE = (0.8, 0.95, 2.0 * np.pi)

        def _lru_scan(lam, Bu):
            lam_b = jnp.broadcast_to(lam, Bu.shape)

            def comb(a, b):
                return (a[0] * b[0], b[0] * a[1] + b[1])
            _, states = jax.lax.associative_scan(comb, (lam_b, Bu), axis=1)
            return states

        def _reference_tuple_inner(x3d, nu_log, theta_log, B_re, B_im, C_re, C_im, D_mat, W1, W2, res_logit):
            lam = jnp.exp(-jnp.exp(nu_log) + 1j * jnp.exp(theta_log))
            gamma = jnp.sqrt(1.0 - jnp.abs(lam) ** 2)
            Bn = gamma[:, None] * (B_re + 1j * B_im)
            Bu = jnp.einsum('bld,nd->bln', x3d.astype(jnp.complex64), Bn)
            states = _lru_scan(lam.astype(jnp.complex64), Bu)
            y = jnp.einsum('bln,mn->blm', states, C_re + 1j * C_im).real + jnp.einsum('bld,md->blm', x3d, D_mat)
            z = jax.nn.gelu(y @ W1) @ W2
            out = x3d + jax.nn.sigmoid(res_logit) * z
            st = states[:, -1]
            return (out, st)
        key = jax.random.key(seed)
        ks = jax.random.split(key, 10)
        u1 = jax.random.uniform(ks[0], (D_STATE,))
        u2 = jax.random.uniform(ks[1], (D_STATE,))
        nu_log = jnp.log(-0.5 * jnp.log(u1 * (RMAX ** 2 - RMIN ** 2) + RMIN ** 2))
        theta_log = jnp.log(MAX_PHASE * u2)
        B_re = jax.random.normal(ks[2], (D_STATE, D_MODEL)) / np.sqrt(2.0 * D_MODEL)
        B_im = jax.random.normal(ks[3], (D_STATE, D_MODEL)) / np.sqrt(2.0 * D_MODEL)
        C_re = jax.random.normal(ks[4], (D_MODEL, D_STATE)) / np.sqrt(D_STATE)
        C_im = jax.random.normal(ks[5], (D_MODEL, D_STATE)) / np.sqrt(D_STATE)
        D_mat = jax.random.normal(ks[6], (D_MODEL, D_MODEL)) / np.sqrt(D_MODEL)
        W1 = jax.random.normal(ks[7], (D_MODEL, D_HIDDEN)) * np.sqrt(2.0 / D_MODEL)
        W2 = jax.random.normal(ks[8], (D_HIDDEN, D_MODEL)) * np.sqrt(2.0 / D_HIDDEN)
        res_logit = jnp.asarray(-1.0, dtype=jnp.float32)
        x3d = jax.random.normal(ks[9], (B, L, D_MODEL), dtype=jnp.float32)
        return {'x3d': x3d, 'nu_log': nu_log, 'theta_log': theta_log, 'B_re': B_re, 'B_im': B_im, 'C_re': C_re, 'C_im': C_im, 'D_mat': D_mat, 'W1': W1, 'W2': W2, 'res_logit': res_logit}
    _L0_attn_in = _L0_attn_setup()

    def _L0_ffn_setup():
        import jax, jax.numpy as jnp
        import numpy as np
        TOP_K = 2
        key = jax.random.key(seed)
        ks = jax.random.split(key, 6)
        B, S, D, E, H = (4, 256, 128, 8, 512)
        x = jax.random.normal(ks[0], (B, S, D), dtype=jnp.float32)
        Wg = jax.random.normal(ks[1], (D, E), dtype=jnp.float32) * 0.02
        W1 = jax.random.normal(ks[2], (E, D, H), dtype=jnp.float32) * 0.02
        b1 = jnp.zeros((E, H), dtype=jnp.float32)
        W2 = jax.random.normal(ks[3], (E, H, D), dtype=jnp.float32) * 0.02
        b2 = jnp.zeros((E, D), dtype=jnp.float32)
        return {'x': x, 'Wg': Wg, 'W1': W1, 'b1': b1, 'W2': W2, 'b2': b2}
    _L0_ffn_in = _L0_ffn_setup()
    _d = {'L0_attn_x3d': _L0_attn_in['x3d'], 'L0_attn_nu_log': _L0_attn_in['nu_log'], 'L0_attn_theta_log': _L0_attn_in['theta_log'], 'L0_attn_B_re': _L0_attn_in['B_re'], 'L0_attn_B_im': _L0_attn_in['B_im'], 'L0_attn_C_re': _L0_attn_in['C_re'], 'L0_attn_C_im': _L0_attn_in['C_im'], 'L0_attn_D_mat': _L0_attn_in['D_mat'], 'L0_attn_W1': _L0_attn_in['W1'], 'L0_attn_W2': _L0_attn_in['W2'], 'L0_attn_res_logit': _L0_attn_in['res_logit'], 'L0_ffn_Wg': _L0_ffn_in['Wg'], 'L0_ffn_W1': _L0_ffn_in['W1'], 'L0_ffn_b1': _L0_ffn_in['b1'], 'L0_ffn_W2': _L0_ffn_in['W2'], 'L0_ffn_b2': _L0_ffn_in['b2']}
    _x0 = _d['L0_attn_x3d']
    _d['L0_attn_x3d'] = jax.random.normal(jax.random.fold_in(jax.random.key(seed), 1), (16, 256, 128), dtype=_x0.dtype)
    del _x0
    return _d

def reference(L0_attn_x3d, L0_attn_nu_log, L0_attn_theta_log, L0_attn_B_re, L0_attn_B_im, L0_attn_C_re, L0_attn_C_im, L0_attn_D_mat, L0_attn_W1, L0_attn_W2, L0_attn_res_logit, L0_ffn_Wg, L0_ffn_W1, L0_ffn_b1, L0_ffn_W2, L0_ffn_b2):

    def _L0_attn_ref(x3d, nu_log, theta_log, B_re, B_im, C_re, C_im, D_mat, W1, W2, res_logit):
        import jax, jax.numpy as jnp
        import numpy as np
        B, L, D_MODEL, D_STATE, D_HIDDEN = (4, 512, 128, 32, 512)
        RMIN, RMAX, MAX_PHASE = (0.8, 0.95, 2.0 * np.pi)

        def _lru_scan(lam, Bu):
            lam_b = jnp.broadcast_to(lam, Bu.shape)

            def comb(a, b):
                return (a[0] * b[0], b[0] * a[1] + b[1])
            _, states = jax.lax.associative_scan(comb, (lam_b, Bu), axis=1)
            return states

        def _reference_tuple_inner(x3d, nu_log, theta_log, B_re, B_im, C_re, C_im, D_mat, W1, W2, res_logit):
            lam = jnp.exp(-jnp.exp(nu_log) + 1j * jnp.exp(theta_log))
            gamma = jnp.sqrt(1.0 - jnp.abs(lam) ** 2)
            Bn = gamma[:, None] * (B_re + 1j * B_im)
            Bu = jnp.einsum('bld,nd->bln', x3d.astype(jnp.complex64), Bn)
            states = _lru_scan(lam.astype(jnp.complex64), Bu)
            y = jnp.einsum('bln,mn->blm', states, C_re + 1j * C_im).real + jnp.einsum('bld,md->blm', x3d, D_mat)
            z = jax.nn.gelu(y @ W1) @ W2
            out = x3d + jax.nn.sigmoid(res_logit) * z
            st = states[:, -1]
            return (out, st)
        return _reference_tuple_inner(x3d, nu_log, theta_log, B_re, B_im, C_re, C_im, D_mat, W1, W2, res_logit)[0]

    def _L0_ffn_ref(x, Wg, W1, b1, W2, b2):
        import jax, jax.numpy as jnp
        import numpy as np
        TOP_K = 2
        B, S, D = x.shape
        E = Wg.shape[1]
        xf = x.reshape(-1, D)
        T = xf.shape[0]
        logits = xf @ Wg
        probs = jax.nn.softmax(logits, axis=-1)
        weights, indices = jax.lax.top_k(probs, TOP_K)
        cw = jnp.zeros((T, E), dtype=x.dtype).at[jnp.arange(T)[:, None], indices].set(weights)
        out = jnp.zeros_like(xf)
        for e in range(E):
            h = jax.nn.gelu(xf @ W1[e] + b1[e], approximate=False)
            y = h @ W2[e] + b2[e]
            out = out + y * cw[:, e:e + 1]
        return out.reshape(B, S, D)
    x = L0_attn_x3d
    x = _layernorm(x + _L0_attn_ref(x, L0_attn_nu_log, L0_attn_theta_log, L0_attn_B_re, L0_attn_B_im, L0_attn_C_re, L0_attn_C_im, L0_attn_D_mat, L0_attn_W1, L0_attn_W2, L0_attn_res_logit), axis=-1)
    x = _layernorm(x + _L0_ffn_ref(x, L0_ffn_Wg, L0_ffn_W1, L0_ffn_b1, L0_ffn_W2, L0_ffn_b2), axis=-1)
    return x

_drawn_inputs = setup_inputs


def setup_inputs(seed=0):
    import zlib

    import numpy as np

    out = dict(_drawn_inputs(seed))
    spreads = {'L0_ffn_b1': (0.0, 0.8), 'L0_ffn_b2': (0.0, 0.36)}
    factors = {'L0_ffn_W1': 4.673, 'L0_ffn_W2': 4.239}
    for name, (base, spread) in spreads.items():
        noise = np.random.default_rng([zlib.crc32(name.encode()), seed]).standard_normal(out[name].shape)
        drawn = base * np.exp(spread * noise) if base else spread * noise
        out[name] = jnp.asarray(drawn.astype(out[name].dtype))
    for name, factor in factors.items():
        out[name] = (out[name] * factor).astype(out[name].dtype)
    return out
```

```python
from contextlib import ExitStack

import concourse.bass as bass
from concourse import mybir

P = 128
F32 = mybir.dt.float32
F32R = mybir.dt.float32r
U32 = mybir.dt.uint32
I32 = mybir.dt.int32
ALU = mybir.AluOpType
ACT = mybir.ActivationFunctionType
AX_X = mybir.AxisListType.X

D = 128
NS = 32
H = 512
HB = H // P
E = 8
CHUNK = 512
QT = CHUNK // P
ROW = D + 2
EPS = 1e-5
ROUND = 1.5 * 2.0**23
ROUND15 = 1.5 * 2.0**8
TWO_PI = 6.283185
BIG = 3.0e38
PARTS = (4, 4)
RING = 4


def wait(eng, sem, value):
    if isinstance(value, int) and value <= 0:
        return
    eng.wait_ge(sem, value)


def build(nc, x, nu_log, theta_log, B_re, B_im, C_re, C_im, D_mat, W1, W2, res_logit,
          Wg, FW1, fb1, FW2, fb2, out):
    NSEQ, S, _ = x.shape
    T = NSEQ * S
    NCH = T // CHUNK
    NT = T // P
    assert sum(PARTS) == NCH
    tiles = [QT * n for n in PARTS]
    slots = [-(-(2 * n + E - 1) // RING) * RING for n in tiles]
    tile0 = [0, tiles[0]]
    slot0 = [0, slots[0]]
    MT = sum(slots)
    MMAX = max(slots)
    NTP = max(tiles)
    starts = [0, PARTS[0]]

    x_t = x.rearrange("b s d -> (b s) d").rearrange("(c q p) d -> c p q d", q=QT, p=P)
    out_t = out.rearrange("b s d -> (b s) d").rearrange("(c q p) d -> c p q d", q=QT, p=P)

    ctx = ExitStack()
    with ctx:
        def sb(name, shape, dt=F32):
            return ctx.enter_context(nc.sbuf_tensor(name, shape, dt))

        def sem(name):
            return ctx.enter_context(nc.semaphore(name))

        slots_d = nc.dram_tensor("slots_d", [MT * P, ROW], F32, kind="Internal").ap()
        results_d = nc.dram_tensor("results_d", [2 * T + MT * P, D], F32, kind="Internal").ap()

        bank = [ctx.enter_context(nc.psum_tensor(f"bank{i}", [P, 512], F32)) for i in range(8)]
        XT_PS, BU_PS, Y_PS, Z_PS, X1T_PS, LG_PS = bank[0], bank[1], bank[2], bank[5], bank[6], bank[7]
        H_PS = [bank[3], bank[4]]
        PRE_PS, HT_PS, XTB_PS, YB_PS = [bank[3], bank[4]], [bank[1], bank[2]], bank[0], [bank[5], bank[6]]

        ident = sb("ident", [P, P])
        ones = sb("ones", [P, P])
        before = sb("before", [P, P])
        steps = sb("steps", [P, S])
        rev = sb("rev", [P, E])
        tok = sb("tok", [P, NT])
        dump = sb("dump", [P, MT])
        jio = sb("jio", [P, MMAX])
        rowmod = sb("rowmod", [P, 1])
        restart = sb("restart", [P, E * NTP])
        zeros = sb("zeros", [P, 4 * ROW])
        base_e = sb("base_e", [P, 4])
        halves = sb("halves", [P, 4])
        minus = sb("minus", [P, 4])
        epss = sb("epss", [P, 8])
        scratch = sb("scratch", [P, 1])
        mhalves = sb("mhalves", [P, 4])
        logs = sb("logs", [P, 2])
        exps = sb("exps", [P, 2])
        negnu = sb("negnu", [P, 1])
        decay = sb("decay", [P, 1])
        om = sb("om", [P, 1])
        gam = sb("gam", [P, 1])
        turn = sb("turn", [P, 4])
        late = sb("late", [P, 4 * CHUNK])
        ph, ph2 = (late[:, n * CHUNK:(n + 1) * CHUNK].rearrange("p (a s) -> p a s", a=2) for n in range(2))
        cs = sb("cs", [P, 2, S])
        tin = sb("tin", [P, S])
        rdec = sb("rdec", [P, 2, S])
        sgl = sb("sgl", [P, 4])
        ball = sb("ball", [P, D])
        cre = sb("cre", [P, NS])
        cim = sb("cim", [P, NS])
        cc = sb("cc", [P, 2, P])
        dm = sb("dm", [P, D])
        bt_h, bt_l = sb("bt_h", [P, P], F32R), sb("bt_l", [P, P], F32R)
        dt_h, dt_l = sb("dt_h", [P, P], F32R), sb("dt_l", [P, P], F32R)
        wcs = sb("wcs", [P, 2, P])
        w1_h, w1_l = sb("w1_h", [P, H], F32R), sb("w1_l", [P, H], F32R)
        w2_h, w2_l = sb("w2_h", [P, HB, D], F32R), sb("w2_l", [P, HB, D], F32R)
        wg = sb("wg", [P, E])
        fst = late[:, 2 * CHUNK:4 * CHUNK].rearrange("p (a h) -> p a h", a=2)
        fw1_h, fw1_l = sb("fw1_h", [P, E * H], F32R), sb("fw1_l", [P, E * H], F32R)
        fw2 = sb("fw2", [P, E * HB, 2 * D], F32R)
        bst = sb("bst", [P, H + D])
        bpk = sb("bpk", [P, H + D], F32R)
        work = sb("work", [P, max(MMAX * D, 10 * CHUNK)])
        pt, ut, qc, qs = (work[:, n * CHUNK:(n + 1) * CHUNK] for n in range(4))
        xr, xres, r1, xn = (work[:, n * CHUNK:(n + 1) * CHUNK].rearrange("p (q d) -> p q d", q=QT) for n in range(4, 8))
        aw_st = work[:, 8 * CHUNK:10 * CHUNK].rearrange("p (a h) -> p a h", a=2)
        yo = work[:, 0:MMAX * D].rearrange("p (m d) -> p m d", m=MMAX)
        xt_h, xt_l = sb("xt_h", [P, 2, CHUNK], F32R), sb("xt_l", [P, 2, CHUNK], F32R)
        y_h, y_l = sb("y_h", [P, CHUNK], F32R), sb("y_l", [P, CHUNK], F32R)
        h32 = sb("h32", [P, 2, CHUNK])
        h_h, h_l = sb("h_h", [P, HB, CHUNK], F32R), sb("h_l", [P, HB, CHUNK], F32R)
        st6 = sb("st6", [P, QT, 6])
        mv = sb("mv", [P, QT, 2])
        var_e = sb("var_e", [P, QT])
        nmean = sb("nmean", [P, QT])
        rstd = sb("rstd", [P, QT])
        nmr = sb("nmr", [P, QT])
        x1t = sb("x1t", [P, CHUNK])
        rows = sb("rows", [P, 2, NT, ROW])
        lg = sb("lg", [P, NT, E])
        m12 = sb("m12", [P, 2, NTP])
        s12 = sb("s12", [P, 2, NTP])
        eq = sb("eq", [P, NTP, E])
        sc = sb("sc", [P, NTP, E])
        oh = sb("oh", [P, 2, NTP, E])
        lg2 = sb("lg2", [P, NTP, E])
        hits = sb("hits", [P, E, NTP])
        incl = sb("incl", [P, E, NTP])
        dst = sb("dst", [P, NTP, E])
        dk = sb("dk", [P, 2, NTP])
        slot_i = sb("slot_i", [P, 2, NT], U32)
        xin = sb("xin", [P, NTP * (E + 1)])
        xex = sb("xex", [P, NTP * (E + 1)])
        den = sb("den", [P, NTP])
        rden = sb("rden", [P, NTP])
        cnt = sb("cnt", [P, 6, E])
        cmp = sb("cmp", [P, MMAX, E])
        ej = sb("ej", [P, MMAX])
        ej7 = sb("ej7", [P, MMAX])
        expert = sb("expert", [P, MT], I32)
        eo = sb("eo", [P, MT])
        hb = h32
        ht_h = [h_h[:, 0, :], h_h[:, 1, :]]
        ht_l = [h_l[:, 0, :], h_l[:, 1, :]]
        xb = sb("xb", [P, RING, ROW])
        xbt_h = [h_h[:, 2, 0:P], h_h[:, 2, P:2 * P]]
        xbt_l = [h_l[:, 2, 0:P], h_l[:, 2, P:2 * P]]
        sel = [h_h[:, 3, k * P:(k + 1) * P] for k in range(RING)]
        ylow = sb("ylow", [P, 2, D])
        dest = sb("dest", [P, MT], U32)
        y01 = late[:, :].rearrange("p (k a q d) -> p k a q d", k=2, a=2, q=QT)
        r2 = sb("r2", [P, QT, D])
        r3 = zeros[:, 0:CHUNK].rearrange("p (q d) -> p q d", q=QT)
        res = sb("res", [P, 2, QT, D])

        names = """zero_ready const_ready par_loaded aw_loaded xr_loaded xres_loaded
            exps_ready negnu_ready decay_ready om_ready gam_ready dve_link pool_link sig_exp cs_ready
            tables_ready ball_ready cc_ready setup_t setup_sb w_ready fw_hi fw_lo
            xT_ready x_hi x_lo bu_ready p_ready u_ready q_ready y_ready y_hi y_lo
            pre_a h_act hh_ready hl_ready z_ready r_ready st_ready mv_ready ve_ready rstd_ready nmr_ready
            xn_ready row0_ready row1_ready x1T_ready x1t_sb lg_ready lg_sb
            hits_ready rank_ready xin_ready xex_ready route_ready
            dispatched prefilled bias_loaded bias_ready
            sel_ready xTb_ready xb_hi xb_lo preb_ready gelu_b hT_ready hth_ready htl_ready
            yb_ready ylow_ready dest_ready yo_ready returned0 returned1
            f_sum f_r f_st f_mv f_ve f_rstd f_nmr f_res""".split()
        sm = {n: sem(n) for n in names}
        fst_loaded = [sem(f"fst_loaded{i}") for i in range(2)]
        xb_loaded = [sem(f"xb_loaded{i}") for i in range(RING)]
        y01_loaded = [sem(f"y01_loaded{i}") for i in range(2)]
        stored = [sem(f"stored{i}") for i in range(2)]

        NFW = 2 * E

        def fw_src(n):
            return FW1[n] if n < E else FW2[n - E].rearrange("(c p) d -> p c d", p=P)

        def fw_stage(n):
            return fst[:, n % 2, :] if n < E else fst[:, n % 2, :].rearrange("p (c d) -> p c d", c=HB)

        def fw_dst(n, part):
            if n < E:
                return (fw1_h, fw1_l)[part][:, n * H:(n + 1) * H]
            return fw2[:, (n - E) * HB:(n - E + 1) * HB, part * D:(part + 1) * D]

        block = ctx.enter_context(nc.Block())

        @block.sync
        def _(sp):
            sp.dma_start(xr[:], x_t[0]).then_inc(sm["xr_loaded"], 16)
            for k in range(4):
                rng = slice(k * NS, (k + 1) * NS)
                sp.dma_start(logs[rng, 0:1], theta_log.rearrange("(n a) -> n a", a=1)).then_inc(sm["par_loaded"], 16)
                sp.dma_start(logs[rng, 1:2], nu_log.rearrange("(n a) -> n a", a=1)).then_inc(sm["par_loaded"], 16)
                sp.dma_start(ball[rng, :], B_re if k in (0, 3) else B_im).then_inc(sm["par_loaded"], 16)
            sp.dma_start(cre[:], C_re).then_inc(sm["par_loaded"], 16)
            sp.dma_start(cim[:], C_im).then_inc(sm["par_loaded"], 16)
            sp.dma_start(dm[:], D_mat).then_inc(sm["par_loaded"], 16)
            sp.dma_start(sgl[:, 0:1], bass.AP(tensor=res_logit.tensor, offset=0, ap=[[0, P], [1, 1]])).then_inc(sm["par_loaded"], 16)
            sp.dma_start(wg[:], Wg).then_inc(sm["par_loaded"], 16)
            sp.dma_start(aw_st[:, 0, :], W1).then_inc(sm["aw_loaded"], 16)
            sp.dma_start(aw_st[:, 1, :].rearrange("p (c d) -> p c d", c=HB),
                         W2.rearrange("(c p) d -> p c d", p=P)).then_inc(sm["aw_loaded"], 16)
            sp.dma_start(xres[:], x_t[0]).then_inc(sm["xres_loaded"], 16)
            sp.wait_ge(sm["zero_ready"], 1)
            n = MT // 4
            sp.dma_start(slots_d.rearrange("(p a b) r -> p a (b r)", p=P, b=4),
                         zeros[:, :].rearrange("p (a n) -> p a n", a=1).to_broadcast([P, n, 4 * ROW])).then_inc(sm["prefilled"], 16)
            sp.wait_ge(sm["zero_ready"], 2)
            for r in (0, NS):
                sp.dma_start(bst[r:r + E, 0:H], fb1).then_inc(sm["bias_loaded"], 16)
                sp.dma_start(bst[r:r + E, H:H + D], fb2).then_inc(sm["bias_loaded"], 16)

            def weights(n):
                wait(sp, sm["fw_lo"], n - 1)
                sp.dma_start(fw_stage(n), fw_src(n)).then_inc(fst_loaded[n % 2], 16)

            for n in range(2):
                weights(n)
            for c in range(1, NCH):
                sp.wait_ge(sm["xT_ready"], c)
                sp.dma_start(xr[:], x_t[c]).then_inc(sm["xr_loaded"], 16)
                sp.wait_ge(sm["r_ready"], c)
                sp.dma_start(xres[:], x_t[c]).then_inc(sm["xres_loaded"], 16)
                for n in range(2 * c, 2 * c + 2):
                    weights(n)

            for p in range(2):
                M, g0 = slots[p], slot0[p]
                sp.wait_ge(sm["dispatched"], 16 * 2 * (tile0[p] + tiles[p]))

                def load(g, k):
                    sp.dma_start(xb[:, k, :], slots_d[bass.ds(g * P, P), :]).then_inc(xb_loaded[k], 16)

                for k in range(RING):
                    wait(sp, sm["yo_ready"], g0 + k - RING + 1)
                    load(g0 + k, k)
                with sp.Fori(1, M // RING) as i:
                    for k in range(RING):
                        sp.wait_ge(sm["yo_ready"], RING * i + (g0 + k - RING + 1))
                        load(RING * i + (g0 + k), k)

            def results(c, k):
                for a in range(2):
                    src = results_d[bass.ds(c * CHUNK + a * T, CHUNK), :].rearrange("(q p) d -> p q d", p=P)
                    sp.dma_start(y01[:, k, a], src).then_inc(y01_loaded[k], 16)

            def store(c, k):
                sp.dma_start(out_t[c] if isinstance(c, int) else
                             out_t[bass.ds(c, 1)].rearrange("a p q d -> (a p) q d"), res[:, k]).then_inc(stored[k], 16)

            sp.wait_ge(sm["returned0"], 16 * slots[0])
            sp.wait_ge(sm["returned1"], 16 * slots[1])
            for k in range(2):
                results(k, k)
            with sp.Fori(0, NCH // 2 - 1) as i:
                for k in range(2):
                    sp.wait_ge(sm["f_res"], 2 * i + (k + 1))
                    store(2 * i + k, k)
                    results(2 * i + (k + 2), k)
            for k in range(2):
                sp.wait_ge(sm["f_res"], NCH - 1 + k)
                store(NCH - 2 + k, k)
            for k in range(2):
                sp.wait_ge(stored[k], 16 * (NCH // 2))
            sp.wait_ge(sm["prefilled"], 16)

        @block.gpsimd
        def _(pool):
            pool.memset(zeros[:], 0.0).then_inc(sm["zero_ready"], 1)
            pool.memset(bst[:], 0.0).then_inc(sm["zero_ready"], 1)
            pool.memset(ident[:], 0.0).then_inc(sm["pool_link"], 1)
            pool.memset(ones[:], 1.0).then_inc(sm["pool_link"], 1)
            pool.memset(restart[:], 1.0).then_inc(sm["pool_link"], 1)
            pool.memset(base_e[:], 2.718281828459045)
            pool.memset(halves[:], 0.5)
            pool.memset(minus[:], -1.0)
            pool.memset(epss[:, 0:4], EPS / 4)
            pool.memset(epss[:, 4:8], EPS)
            pool.memset(mhalves[:], -0.5).then_inc(sm["pool_link"], 1)
            pool.iota(steps[:], [[1, S]], base=0, channel_multiplier=0, allow_small_or_imprecise_dtypes=True).then_inc(sm["const_ready"], 1)
            pool.wait_ge(sm["par_loaded"], 16 * 17)
            pool.wait_ge(sm["pool_link"], 4)
            pool.tensor_tensor(exps[:], base_e[:, 0:2], logs[:], ALU.pow).then_inc(sm["exps_ready"], 1)
            pool.wait_ge(sm["exps_ready"], 1)
            pool.tensor_scalar(negnu[:], exps[:, 1:2], -1.0, None, ALU.mult).then_inc(sm["negnu_ready"], 1)
            pool.wait_ge(sm["negnu_ready"], 1)
            pool.tensor_tensor(decay[:], base_e[:, 0:1], negnu[:], ALU.pow).then_inc(sm["decay_ready"], 1)
            pool.wait_ge(sm["om_ready"], 1)
            pool.tensor_tensor(gam[:], om[:], halves[:, 0:1], ALU.pow).then_inc(sm["gam_ready"], 1)
            pool.affine_select(out=ident[:], in_=ident[:], compare_op=ALU.not_equal, fill=1.0, base=0,
                               pattern=[[-1, P]], channel_multiplier=1).then_inc(sm["const_ready"], 1)
            for a, b, src, sign in ((0, 0, cre, 1.0), (0, 1, cim, -1.0), (1, 0, cim, -1.0), (1, 1, cre, -1.0)):
                dstv = cc[:, a, :].rearrange("p (r b n) -> p r b n", r=2, b=2)[:, :, b, :]
                pool.tensor_scalar(dstv, src[:, :].rearrange("p (a n) -> p a n", a=1).to_broadcast([P, 2, NS]),
                                   sign, None, ALU.mult).then_inc(sm["cc_ready"], 1)
            pool.affine_select(out=before[:], in_=ones[:], compare_op=ALU.is_gt, fill=0.0, base=0,
                               pattern=[[1, P]], channel_multiplier=-1).then_inc(sm["const_ready"], 1)
            pool.iota(rev[:], [[-1, E]], base=E, channel_multiplier=0, allow_small_or_imprecise_dtypes=True)
            pool.iota(tok[:], [[P, NT]], base=0, channel_multiplier=1, allow_small_or_imprecise_dtypes=True)
            pool.iota(dump[:], [[P, MT]], base=2 * T, channel_multiplier=1, allow_small_or_imprecise_dtypes=True)
            pool.iota(jio[:], [[1, MMAX]], base=0, channel_multiplier=0, allow_small_or_imprecise_dtypes=True)
            pool.iota(rowmod[:], [[0, 1]], base=0, channel_multiplier=1, allow_small_or_imprecise_dtypes=True)
            pool.wait_ge(sm["pool_link"], 3)
            pool.memset(restart[:, :].rearrange("p (e t) -> p e t", e=E)[:, :, 0:1], 0.0).then_inc(sm["const_ready"], 1)

            def weights(n):
                pool.wait_ge(sm["fw_hi"], n + 1)
                pool.tensor_tensor(fw_dst(n, 1), fw_stage(n), fw_dst(n, 0).bitcast(F32), ALU.subtract).then_inc(sm["fw_lo"], 1)

            def norm(c):
                pool.wait_ge(sm["mv_ready"], QT * (c + 1))
                wait(pool, sm["xn_ready"], c)
                pool.tensor_tensor(var_e[:], mv[:, :, 1], epss[:, 0:4], ALU.add).then_inc(sm["ve_ready"], 1)
                pool.tensor_tensor(nmean[:], mv[:, :, 0], minus[:], ALU.mult)
                pool.wait_ge(sm["ve_ready"], c + 1)
                pool.tensor_tensor(rstd[:], var_e[:], mhalves[:], ALU.pow).then_inc(sm["rstd_ready"], 1)
                pool.wait_ge(sm["rstd_ready"], c + 1)
                pool.tensor_tensor(nmr[:], nmean[:], rstd[:], ALU.mult).then_inc(sm["nmr_ready"], 1)
                pool.wait_ge(sm["xn_ready"], c + 1)
                pool.tensor_copy(rows[:, 1, bass.ds(QT * c, QT), 0:D], xn[:]).then_inc(sm["row1_ready"], 1)

            def dispatch(i):
                for k in range(2):
                    pool.indirect_dma_start(out=slots_d, out_offset=bass.IndirectOffsetOnAxis(ap=slot_i[:, k, i:i + 1], axis=0),
                                            in_=rows[:, k, i, :], in_offset=None).then_inc(sm["dispatched"], 16)

            def send_back(p, j):
                g = slot0[p] + j
                pool.wait_ge(sm["yo_ready"], g + 1)
                pool.indirect_dma_start(out=results_d, out_offset=bass.IndirectOffsetOnAxis(ap=dest[:, g:g + 1], axis=0),
                                        in_=yo[:, j, :], in_offset=None).then_inc(sm[f"returned{p}"], 16)

            first = 0
            for c in range(NCH):
                for n in range(2 * c, 2 * c + 2):
                    weights(n)
                if c > PARTS[0]:
                    if c == PARTS[0] + 1:
                        pool.wait_ge(sm["prefilled"], 16)
                        pool.wait_ge(sm["route_ready"], 1)
                    last = tiles[0] * (c - PARTS[0]) // (PARTS[1] - 1)
                    for i in range(first, last):
                        dispatch(i)
                    first = last
                norm(c)
            pool.wait_ge(sm["route_ready"], 2)
            todo = [("d", i) for i in range(tile0[1], NT)]
            for j in range(slots[0]):
                if todo and j >= 1:
                    dispatch(todo.pop(0)[1])
                send_back(0, j)
            for _, i in todo:
                dispatch(i)
            for j in range(slots[1]):
                send_back(1, j)

            def final_norm(c):
                pool.wait_ge(sm["f_mv"], QT * (c + 1))
                wait(pool, sm["f_res"], c)
                pool.tensor_tensor(var_e[:], mv[:, :, 1], epss[:, 4:8], ALU.add).then_inc(sm["f_ve"], 1)
                pool.tensor_tensor(nmean[:], mv[:, :, 0], minus[:], ALU.mult)
                pool.wait_ge(sm["f_ve"], c + 1)
                pool.tensor_tensor(rstd[:], var_e[:], mhalves[:], ALU.pow).then_inc(sm["f_rstd"], 1)
                pool.wait_ge(sm["f_rstd"], c + 1)
                pool.tensor_tensor(nmr[:], nmean[:], rstd[:], ALU.mult).then_inc(sm["f_nmr"], 1)

            final_norm(0)
            with pool.Fori(1, NCH) as c:
                final_norm(c)

        @block.scalar
        def _(act):
            act.wait_ge(sm["par_loaded"], 16 * 17)
            act.activation(sgl[:, 1:2], sgl[:, 0:1], ACT.Exp, scale=-1.0).then_inc(sm["sig_exp"], 1)
            act.wait_ge(sm["tables_ready"], 1)
            act.activation(cs[:, :, :].rearrange("p a s -> p (a s)"), ph[:, :, :].rearrange("p a s -> p (a s)"),
                           ACT.Sin, scale=TWO_PI).then_inc(sm["cs_ready"], 1)
            act.preload_act_table_set("gelu_apprx_tanh_and_others")

            def weights(n):
                act.wait_ge(fst_loaded[n % 2], 16 * (n // 2 + 1))
                act.copy(fw_dst(n, 0), fw_stage(n)).then_inc(sm["fw_hi"], 1)

            def x_high(c):
                act.wait_ge(sm["xT_ready"], c + 1)
                wait(act, sm["y_ready"], c - 1)
                act.copy(xt_h[:, c % 2, :] if isinstance(c, int) else xt_h[:, bass.ds(c % 2, 1), :].rearrange("p a n -> p (a n)"),
                         XT_PS[:]).then_inc(sm["x_hi"], 1)

            def chunk(c, more, before_):
                if more:
                    x_high(c + 1)
                act.wait_ge(sm["y_ready"], c + 1)
                wait(act, sm["pre_a"], HB * c)
                act.copy(y_h[:], Y_PS[:]).then_inc(sm["y_hi"], 1)
                if before_:
                    act.wait_ge(sm["x1T_ready"], c)
                    wait(act, sm["lg_ready"], c - 1)
                    act.copy(x1t[:], X1T_PS[:]).then_inc(sm["x1t_sb"], 1)

                def high(b):
                    act.wait_ge(sm["h_act"], HB * c + b + 1)
                    wait(act, sm["z_ready"], c)
                    act.copy(h_h[:, b, :], h32[:, b % 2, :]).then_inc(sm["hh_ready"], 1)

                for b in range(HB):
                    act.wait_ge(sm["pre_a"], HB * c + b + 1)
                    wait(act, sm["hl_ready"], HB * c + b - 1)
                    act.activation(h32[:, b % 2, :], H_PS[b % 2][:], ACT.Gelu_apprx_tanh).then_inc(sm["h_act"], 1)
                    high(b)

            def norm(c):
                act.wait_ge(sm["nmr_ready"], c + 1)
                wait(act, sm["x1T_ready"], c)
                wait(act, sm["row1_ready"], c)
                for q in range(QT):
                    last = act.activation(xn[:, q, :], r1[:, q, :], ACT.Identity, bias=nmr[:, q:q + 1], scale=rstd[:, q:q + 1])
                last.then_inc(sm["xn_ready"], 1)
                act.wait_ge(sm["xn_ready"], c + 1)
                act.copy(rows[:, 0, bass.ds(QT * c, QT), 0:D], xn[:]).then_inc(sm["row0_ready"], 1)

            def tail(c):
                act.wait_ge(sm["x1T_ready"], c + 1)
                wait(act, sm["lg_ready"], c)
                act.copy(x1t[:], X1T_PS[:]).then_inc(sm["x1t_sb"], 1)

            def softmax_exp(p):
                act.wait_ge(sm["xin_ready"], p + 1)
                n = tiles[p] * (E + 1)
                act.activation(xex[:, 0:n], xin[:, 0:n], ACT.Exp).then_inc(sm["xex_ready"], 1)

            x_high(0)
            chunk(0, True, False)
            for n in range(4):
                weights(n)
            norm(0)
            for c in range(1, NCH):
                chunk(c, c < NCH - 1, True)
                for n in range(2 * c + 2, min(2 * c + 4, NFW)):
                    weights(n)
                norm(c)
                if c == PARTS[0]:
                    softmax_exp(0)
                    act.preload_act_table_set("gelu_apprx_tanh_and_others")
            tail(NCH - 1)
            softmax_exp(1)
            act.preload_act_table_set("gelu_and_others")

            def step(p, s, k, g, acts):
                if acts[0]:
                    act.wait_ge(sm["preb_ready"], g + 1)
                    wait(act, sm["hT_ready"], g - 1)
                    act.activation(hb[:, k % 2, :], PRE_PS[k % 2][:], ACT.Gelu).then_inc(sm["gelu_b"], 1)
                if acts[1]:
                    act.wait_ge(sm["hT_ready"], g)
                    wait(act, sm["yb_ready"], g - 2)
                    act.copy(ht_h[(k - 1) % 2], HT_PS[(k - 1) % 2][:]).then_inc(sm["hth_ready"], 1)
                if acts[2]:
                    act.wait_ge(sm["yb_ready"], g - 1)
                    wait(act, sm["yo_ready"], g - 3)
                    act.activation(ylow[:, k % 2, :], YB_PS[k % 2][:, D:2 * D], ACT.Copy,
                                   scale=xb[:, (k - 2) % 4, D + 1:D + 2]).then_inc(sm["ylow_ready"], 1)

            for p in range(2):
                walk(act, p, slots[p], slot0[p], step)

            act.wait_ge(sm["f_r"], 1)

            def final_apply(c, k):
                act.wait_ge(sm["f_nmr"], c + 1)
                wait(act, stored[k], 8 * (c - k))
                for q in range(QT):
                    last = act.activation(res[:, k, q, :], r3[:, q, :], ACT.Identity, bias=nmr[:, q:q + 1], scale=rstd[:, q:q + 1])
                last.then_inc(sm["f_res"], 1)

            for k in range(2):
                final_apply(k, k)
            with act.Fori(1, NCH // 2) as i:
                for k in range(2):
                    final_apply(2 * i + k, k)

        @block.vector
        def _(dve):
            chain = [0]

            def link(ins):
                chain[0] += 1
                ins.then_inc(sm["dve_link"], 1)
                dve.wait_ge(sm["dve_link"], chain[0])

            dve.wait_ge(sm["exps_ready"], 1)
            link(dve.tensor_scalar(turn[:, 0:1], exps[:, 0:1], 0.15915494309189535, None, ALU.mult))
            link(dve.tensor_scalar(turn[:, 1:2], turn[:, 0:1], ROUND, -ROUND, ALU.add, ALU.add))
            link(dve.tensor_tensor(turn[:, 0:1], turn[:, 0:1], turn[:, 1:2], ALU.subtract))
            link(dve.tensor_scalar(turn[:, 2:3], turn[:, 0:1], ROUND15, -ROUND15, ALU.add, ALU.add))
            link(dve.tensor_tensor(turn[:, 3:4], turn[:, 0:1], turn[:, 2:3], ALU.subtract))
            dve.wait_ge(sm["const_ready"], 1)
            link(dve.tensor_scalar(ph[:, 0, :], steps[:], turn[:, 2:3], None, ALU.mult))
            link(dve.tensor_scalar(ph2[:, 0, :], ph[:, 0, :], ROUND, -ROUND, ALU.add, ALU.add))
            link(dve.tensor_tensor(ph[:, 1, :], ph[:, 0, :], ph2[:, 0, :], ALU.subtract))
            link(dve.scalar_tensor_tensor(out=ph2[:, 1, :], in0=steps[:], scalar=turn[:, 3:4], in1=ph[:, 1, :], op0=ALU.mult, op1=ALU.add))
            dve.tensor_scalar(ph2[:, 0, :], ph2[:, 1, :], 0.25, None, ALU.add)
            dve.wait_ge(sm["decay_ready"], 1)
            link(dve.tensor_tensor(om[:], decay[:], decay[:], ALU.mult))
            dve.tensor_scalar(om[:], om[:], -1.0, 1.0, ALU.mult, ALU.add).then_inc(sm["om_ready"], 1)
            link(dve.tensor_scalar(cs[:, :, :], ph2[:, :, :], ROUND, -ROUND, ALU.add, ALU.add))
            dve.tensor_tensor(ph[:, :, :], ph2[:, :, :], cs[:, :, :], ALU.subtract).then_inc(sm["tables_ready"], 1)
            link(dve.tensor_scalar(rdec[:, :, :], ph2[:, :, :], 0.0, decay[:, 0:1], ALU.mult, ALU.add))
            link(dve.memset(rdec[:, :, 0:1], 0.0))
            dve.wait_ge(sm["gam_ready"], 1)
            for a, b in ((0, 96), (96, 128)):
                pass
            link(dve.tensor_scalar(ball[:], ball[:], gam[:, 0:1], None, ALU.mult))
            dve.tensor_scalar(ball[96:P, :], ball[96:P, :], -1.0, None, ALU.mult).then_inc(sm["ball_ready"], 1)
            dve.wait_ge(sm["aw_loaded"], 32)
            dve.tensor_copy(w1_h[:], aw_st[:, 0, :])
            link(dve.tensor_copy(w2_h[:, :, :].rearrange("p c d -> p (c d)"), aw_st[:, 1, :]))
            dve.tensor_tensor(w1_l[:], aw_st[:, 0, :], w1_h[:].bitcast(F32), ALU.subtract)
            dve.tensor_tensor(w2_l[:, :, :].rearrange("p c d -> p (c d)"), aw_st[:, 1, :],
                              w2_h[:, :, :].rearrange("p c d -> p (c d)").bitcast(F32), ALU.subtract).then_inc(sm["w_ready"], 1)
            dve.wait_ge(sm["sig_exp"], 1)
            link(dve.tensor_scalar(sgl[:, 2:3], sgl[:, 1:2], 1.0, None, ALU.add))
            link(dve.reciprocal(sgl[:, 3:4], sgl[:, 2:3]))
            link(dve.tensor_scalar(sgl[:, 2:3], sgl[:, 3:4], 0.5, None, ALU.mult))
            dve.wait_ge(sm["setup_t"], 1)
            dve.tensor_copy(bt_h[:], Z_PS[:, 0:P])
            dve.tensor_copy(dt_h[:], Z_PS[:, P:2 * P])
            link(dve.tensor_copy(wcs[:, :, :].rearrange("p a n -> p (a n)"), Z_PS[:, 2 * P:4 * P]))
            dve.tensor_tensor(bt_l[:], Z_PS[:, 0:P], bt_h[:].bitcast(F32), ALU.subtract)
            dve.tensor_tensor(dt_l[:], Z_PS[:, P:2 * P], dt_h[:].bitcast(F32), ALU.subtract).then_inc(sm["setup_sb"], 1)
            dve.wait_ge(sm["cs_ready"], 1)
            dve.tensor_copy(tin[0:64, :], cs[0:64, 0, :])
            link(dve.tensor_copy(tin[64:P, :], cs[64:P, 1, :]))

            def both(t):
                return t.rearrange("p (a s) -> p a s", a=1).to_broadcast([P, 2, S])

            def two(t):
                return t.rearrange("p (a s) -> p a s", a=2)

            def x_low(c):
                dve.wait_ge(sm["x_hi"], c + 1)
                ix = (lambda t: t[:, c % 2, :]) if isinstance(c, int) else (lambda t: t[:, bass.ds(c % 2, 1), :].rearrange("p a n -> p (a n)"))
                dve.tensor_tensor(ix(xt_l), XT_PS[:], ix(xt_h).bitcast(F32), ALU.subtract).then_inc(sm["x_lo"], 1)

            def states(c):
                dve.wait_ge(sm["bu_ready"], c + 1)
                dve.tensor_tensor(two(pt[:, :]), two(BU_PS[:, :]), both(tin[:, :]), ALU.mult).then_inc(sm["p_ready"], 1)
                dve.wait_ge(sm["p_ready"], c + 1)
                dve.tensor_tensor_scan(ut[:], rdec[:, :, :].rearrange("p a s -> p (a s)"), pt[:], 0.0, ALU.mult, ALU.add).then_inc(sm["u_ready"], 1)
                dve.wait_ge(sm["u_ready"], c + 1)
                wait(dve, sm["y_ready"], c)
                dve.tensor_tensor(two(qc[:, :]), two(ut[:, :]), both(cs[:, 0, :]), ALU.mult)
                dve.tensor_tensor(two(qs[:, :]), two(ut[:, :]), both(cs[:, 1, :]), ALU.mult).then_inc(sm["q_ready"], 1)

            def chunk(c, more, before_):
                if more:
                    x_low(c + 1)
                    states(c + 1)
                dve.wait_ge(sm["y_hi"], c + 1)
                dve.tensor_tensor(y_l[:], Y_PS[:], y_h[:].bitcast(F32), ALU.subtract).then_inc(sm["y_lo"], 1)
                for b in range(HB):
                    dve.wait_ge(sm["hh_ready"], HB * c + b + 1)
                    dve.tensor_tensor(h_l[:, b, :], h32[:, b % 2, :], h_h[:, b, :].bitcast(F32), ALU.subtract).then_inc(sm["hl_ready"], 1)
                if before_:
                    logits(c - 1)
                dve.wait_ge(sm["z_ready"], c + 1)
                dve.wait_ge(sm["xres_loaded"], 16 * (c + 1))
                wait(dve, sm["xn_ready"], c)
                dve.scalar_tensor_tensor(out=r1[:, :, :].rearrange("p q d -> p (q d)"), in0=Z_PS[:], scalar=sgl[:, 2:3],
                                         in1=xres[:, :, :].rearrange("p q d -> p (q d)"), op0=ALU.mult, op1=ALU.add).then_inc(sm["r_ready"], 1)
                dve.wait_ge(sm["r_ready"], c + 1)
                for q in range(QT):
                    dve.bn_stats(st6[:, q, :], r1[:, q, :]).then_inc(sm["st_ready"], 1)
                wait(dve, sm["nmr_ready"], c)
                for q in range(QT):
                    dve.wait_ge(sm["st_ready"], QT * c + q + 1)
                    dve.bn_aggr(mv[:, q, :], st6[:, q, :]).then_inc(sm["mv_ready"], 1)

            def logits(c):
                dve.wait_ge(sm["lg_ready"], c + 1)
                dve.tensor_copy(lg[:, bass.ds(QT * c, QT), :].rearrange("p q e -> p (q e)"), LG_PS[:, 0:QT * E]).then_inc(sm["lg_sb"], 1)

            def route(p):
                n, t0, M, g0 = tiles[p], tile0[p], slots[p], slot0[p]
                lgp = lg[:, t0:t0 + n, :]
                dve.wait_ge(sm["lg_sb"], starts[p] + PARTS[p])

                def over_e(t):
                    return t.rearrange("p (n a) -> p n a", a=1).to_broadcast([P, n, E])

                for k in range(2):
                    src = lgp if k == 0 else lg2[:, 0:n, :]
                    link(dve.tensor_reduce(m12[:, k, 0:n], src, AX_X, ALU.max))
                    link(dve.tensor_tensor(eq[:, 0:n, :], src, over_e(m12[:, k, 0:n]), ALU.is_equal))
                    link(dve.tensor_tensor(sc[:, 0:n, :], eq[:, 0:n, :], rev[:, :].rearrange("p (a e) -> p a e", a=1).to_broadcast([P, n, E]), ALU.mult))
                    link(dve.tensor_reduce(s12[:, k, 0:n], sc[:, 0:n, :], AX_X, ALU.max))
                    link(dve.tensor_tensor(oh[:, k, 0:n, :], sc[:, 0:n, :], over_e(s12[:, k, 0:n]), ALU.is_equal))
                    if k == 0:
                        link(dve.scalar_tensor_tensor(out=lg2[:, 0:n, :], in0=oh[:, 0, 0:n, :], scalar=-BIG, in1=lgp, op0=ALU.mult, op1=ALU.add))
                hv = hits[:, :, :].rearrange("p e t -> p (e t)")[:, 0:E * n]
                iv = incl[:, :, :].rearrange("p e t -> p (e t)")[:, 0:E * n]
                link(dve.tensor_tensor(hv.rearrange("p (e t) -> p t e", e=E), oh[:, 0, 0:n, :], oh[:, 1, 0:n, :], ALU.add))
                if n != NTP:
                    rs = restart[:, :].rearrange("p (e t) -> p e t", e=E)[:, :, 0:n]
                    link(dve.tensor_copy(cmp[:, :, :].rearrange("p a b -> p (a b)")[:, 0:E * n].rearrange("p (e t) -> p e t", e=E), rs))
                    rsv = cmp[:, :, :].rearrange("p a b -> p (a b)")[:, 0:E * n]
                else:
                    rsv = restart[:]
                link(dve.tensor_tensor_scan(iv, rsv, hv, 0.0, ALU.mult, ALU.add))
                dve.tensor_copy(cnt[:, 0, :], iv.rearrange("p (e t) -> p e t", e=E)[:, :, n - 1]).then_inc(sm["hits_ready"], 1)
                dve.tensor_tensor(xin[:, 0:n * E].rearrange("p (n e) -> p n e", e=E), lgp, over_e(m12[:, 0, 0:n]), ALU.subtract)
                dve.tensor_tensor(xin[:, n * E:n * (E + 1)], m12[:, 1, 0:n], m12[:, 0, 0:n], ALU.subtract).then_inc(sm["xin_ready"], 1)
                dve.wait_ge(sm["rank_ready"], p + 1)
                link(dve.tensor_scalar(cnt[:, 1, :], LG_PS[:, E:2 * E], 1.0 / P, 63.5 / P, ALU.mult, ALU.add))
                link(dve.tensor_scalar(cnt[:, 2, :], cnt[:, 1, :], ROUND, -ROUND, ALU.add, ALU.add))
                link(dve.tensor_tensor_scan(cnt[:, 3, :], ones[:, 0:E], cnt[:, 2, :], 0.0, ALU.mult, ALU.add))
                link(dve.tensor_tensor(cnt[:, 4, :], cnt[:, 3, :], cnt[:, 2, :], ALU.subtract))
                link(dve.scalar_tensor_tensor(out=cnt[:, 5, :], in0=cnt[:, 4, :], scalar=float(P), in1=LG_PS[:, 0:E], op0=ALU.mult, op1=ALU.add))
                link(dve.tensor_tensor(dst[:, 0:n, :], iv.rearrange("p (e t) -> p t e", e=E),
                                       cnt[:, 5:6, :].to_broadcast([P, n, E]), ALU.add))
                dve.wait_ge(sm["row1_ready"], starts[p] + PARTS[p])
                dve.wait_ge(sm["row0_ready"], starts[p] + PARTS[p])
                off = g0 * P - 1
                for k in range(2):
                    link(dve.tensor_tensor(sc[:, 0:n, :], oh[:, k, 0:n, :], dst[:, 0:n, :], ALU.mult))
                    link(dve.tensor_reduce(dk[:, k, 0:n], sc[:, 0:n, :], AX_X, ALU.add))
                    dve.tensor_scalar(slot_i[:, k, t0:t0 + n], dk[:, k, 0:n], float(off), None, ALU.add)
                    link(dve.scalar_tensor_tensor(out=s12[:, k, 0:n], in0=dk[:, k, 0:n], scalar=-1.0, in1=tok[:, t0:t0 + n], op0=ALU.mult, op1=ALU.add))
                    dve.tensor_scalar(rows[:, k, t0:t0 + n, D], s12[:, k, 0:n], float(k * T - 2 * T - off), None, ALU.add)
                dve.wait_ge(sm["xex_ready"], p + 1)
                link(dve.tensor_reduce(den[:, 0:n], xex[:, 0:n * E].rearrange("p (n e) -> p n e", e=E), AX_X, ALU.add))
                link(dve.reciprocal(rden[:, 0:n], den[:, 0:n]))
                dve.tensor_copy(rows[:, 0, t0:t0 + n, D + 1], rden[:, 0:n])
                link(dve.tensor_tensor(rows[:, 1, t0:t0 + n, D + 1], xex[:, n * E:n * (E + 1)], rden[:, 0:n], ALU.mult))
                link(dve.tensor_tensor(cmp[:, 0:M, :], jio[:, 0:M].rearrange("p (m a) -> p m a", a=1).to_broadcast([P, M, E]),
                                       cnt[:, 3:4, :].to_broadcast([P, M, E]), ALU.is_ge))
                link(dve.tensor_reduce(ej[:, 0:M], cmp[:, 0:M, :], AX_X, ALU.add))
                link(dve.tensor_scalar(ej7[:, 0:M], ej[:, 0:M], float(E - 1), None, ALU.min))
                dve.tensor_copy(expert[:, g0:g0 + M], ej7[:, 0:M])
                dve.tensor_scalar(eo[:, g0:g0 + M], ej7[:, 0:M], rowmod[:, 0:1], None, ALU.is_equal).then_inc(sm["route_ready"], 1)

            x_low(0)
            states(0)
            chunk(0, True, False)
            dve.wait_ge(sm["bias_loaded"], 64)
            link(dve.tensor_copy(bpk[:], bst[:]))
            dve.tensor_tensor(bpk[32:64, :], bst[32:64, :], bpk[32:64, :].bitcast(F32), ALU.subtract).then_inc(sm["bias_ready"], 1)
            dve.wait_ge(sm["const_ready"], 4)
            link(dve.tensor_scalar(rowmod[32:64, :], rowmod[32:64, :], -32.0, None, ALU.add))
            for c in range(1, NCH):
                chunk(c, c < NCH - 1, True)
                if c == PARTS[0]:
                    route(0)
            logits(NCH - 1)
            route(1)

            def split_x(g, k):
                wait(dve, sm["yb_ready"], g - 3)
                eog = eo[:, g:g + 1] if isinstance(g, int) else eo[:, bass.ds(g, 1)]
                dve.tensor_copy(sel[k % 4], eog.to_broadcast([P, P])).then_inc(sm["sel_ready"], 1)
                dve.wait_ge(sm["xTb_ready"], g + 1)
                wait(dve, sm["preb_ready"], g - 1)
                dve.tensor_copy(xbt_h[k % 2], XTB_PS[:, 0:P]).then_inc(sm["xb_hi"], 1)
                dve.wait_ge(sm["xb_hi"], g + 1)
                dve.tensor_tensor(xbt_l[k % 2], XTB_PS[:, 0:P], xbt_h[k % 2].bitcast(F32), ALU.subtract).then_inc(sm["xb_lo"], 1)

            def step(p, s, k, g, acts):
                if p == 0 and isinstance(s, int) and s == 0:
                    dve.wait_ge(sm["z_ready"], NCH)
                if isinstance(s, int) and s == 0:
                    dve.wait_ge(sm["route_ready"], p + 1)
                    split_x(g, k)
                if acts[3]:
                    split_x(g + 1, k + 1)
                if acts[1]:
                    dve.wait_ge(sm["hth_ready"], g)
                    wait(dve, sm["yb_ready"], g - 2)
                    dve.tensor_tensor(ht_l[(k - 1) % 2], HT_PS[(k - 1) % 2][:], ht_h[(k - 1) % 2].bitcast(F32), ALU.subtract).then_inc(sm["htl_ready"], 1)
                if acts[2]:
                    if p == 1 and isinstance(s, int) and s == 2:
                        dve.wait_ge(sm["returned0"], 16 * slots[0])
                    j = s - 2
                    one = lambda t, i: t[:, i:i + 1] if isinstance(i, int) else t[:, bass.ds(i, 1)]
                    yoj = yo[:, j, :] if isinstance(j, int) else yo[:, bass.ds(j, 1), :].rearrange("p a d -> p (a d)")
                    dve.wait_ge(sm["ylow_ready"], g - 1)
                    dve.tensor_tensor(one(dest, g - 2), xb[:, (k - 2) % 4, D:D + 1], one(dump, g - 2), ALU.add)
                    dve.scalar_tensor_tensor(out=yoj, in0=YB_PS[k % 2][:, 0:D], scalar=xb[:, (k - 2) % 4, D + 1:D + 2],
                                             in1=ylow[:, k % 2, :], op0=ALU.mult, op1=ALU.add).then_inc(sm["yo_ready"], 1)

            for p in range(2):
                walk(dve, p, slots[p], slot0[p], step)

            def final(c, k):
                dve.wait_ge(y01_loaded[k], 16 * (c - k) + 32)
                wait(dve, sm["f_st"], QT * c)
                dve.tensor_tensor(r2[:, :, :], y01[:, k, 0], y01[:, k, 1], ALU.add).then_inc(sm["f_sum"], 1)
                dve.wait_ge(sm["f_sum"], c + 1)
                wait(dve, sm["f_res"], c)
                dve.tensor_tensor(r3[:, :, :], r2[:, :, :], rows[:, 0, bass.ds(QT * c, QT), 0:D], ALU.add).then_inc(sm["f_r"], 1)
                dve.wait_ge(sm["f_r"], c + 1)
                for q in range(QT):
                    dve.bn_stats(st6[:, q, :], r3[:, q, :]).then_inc(sm["f_st"], 1)
                dve.wait_ge(sm["f_st"], QT * c + QT)
                dve.memset(scratch[:], 0.0)
                for q in range(QT):
                    dve.bn_aggr(mv[:, q, :], st6[:, q, :]).then_inc(sm["f_mv"], 1)

            for k in range(2):
                final(k, k)
            with dve.Fori(1, NCH // 2) as i:
                for k in range(2):
                    final(2 * i + k, k)

        @block.tensor
        def _(pe):
            mm = pe.matmul
            pe.wait_ge(sm["const_ready"], 2)
            pe.wait_ge(sm["ball_ready"], 1)
            pe.wait_ge(sm["cc_ready"], 4)
            pe.transpose(Z_PS[:, 0:P], ball[:], ident[:])
            pe.transpose(Z_PS[:, P:2 * P], dm[:], ident[:])
            pe.transpose(Z_PS[:, 2 * P:3 * P], cc[:, 0, :], ident[:])
            pe.transpose(Z_PS[:, 3 * P:4 * P], cc[:, 1, :], ident[:]).then_inc(sm["setup_t"], 1)

            def products(out_, wh, wl, xh, xl, start, stop):
                mm(out_, wh, xh, start=start, stop=False)
                mm(out_, wh, xl, start=False, stop=False)
                return mm(out_, wl, xh, start=False, stop=stop)

            def part_of(t, c):
                return t[:, c % 2, :] if isinstance(c, int) else t[:, bass.ds(c % 2, 1), :].rearrange("p a n -> p (a n)")

            def inputs(c):
                pe.wait_ge(sm["xr_loaded"], 16 * (c + 1))
                wait(pe, sm["x_lo"], c)
                for q in range(QT):
                    last = pe.transpose(XT_PS[:, q * P:(q + 1) * P], xr[:, q, :], ident[:])
                last.then_inc(sm["xT_ready"], 1)
                if isinstance(c, int) and c == 0:
                    pe.wait_ge(sm["setup_sb"], 1)
                pe.wait_ge(sm["x_lo"], c + 1)
                wait(pe, sm["p_ready"], c)
                products(BU_PS[:], bt_h[:], bt_l[:], part_of(xt_h, c), part_of(xt_l, c), True, True).then_inc(sm["bu_ready"], 1)

            def transposed(c):
                pe.wait_ge(sm["xn_ready"], c + 1)
                wait(pe, sm["x1t_sb"], c)
                for q in range(QT):
                    last = pe.transpose(X1T_PS[:, q * P:(q + 1) * P], xn[:, q, :], ident[:])
                last.then_inc(sm["x1T_ready"], 1)

            def logits(c):
                pe.wait_ge(sm["x1t_sb"], c + 1)
                wait(pe, sm["lg_sb"], c)
                for q in range(QT):
                    last = mm(LG_PS[:, q * E:(q + 1) * E], x1t[:, q * P:(q + 1) * P], wg[:], start=True, stop=True)
                last.then_inc(sm["lg_ready"], 1)

            def chunk(c, more, before_):
                if more:
                    inputs(c + 1)
                pe.wait_ge(sm["q_ready"], c + 1)
                wait(pe, sm["y_lo"], c)
                mm(Y_PS[:], wcs[:, 0, :], qc[:], start=True, stop=False)
                mm(Y_PS[:], wcs[:, 1, :], qs[:], start=False, stop=False)
                products(Y_PS[:], dt_h[:], dt_l[:], part_of(xt_h, c), part_of(xt_l, c), False, True).then_inc(sm["y_ready"], 1)
                if before_:
                    transposed(c - 1)
                pe.wait_ge(sm["y_lo"], c + 1)
                for b in range(HB):
                    wait(pe, sm["h_act"], HB * c + b - 1)
                    products(H_PS[b % 2][:], w1_h[:, b * P:(b + 1) * P], w1_l[:, b * P:(b + 1) * P], y_h[:], y_l[:],
                             True, True).then_inc(sm["pre_a"], 1)
                if before_:
                    logits(c - 1)
                pe.wait_ge(sm["hl_ready"], HB * (c + 1))
                wait(pe, sm["r_ready"], c)
                for q in range(QT):
                    o = Z_PS[:, q * D:(q + 1) * D]
                    for b in range(HB):
                        hh, hl = h_h[:, b, q * P:(q + 1) * P], h_l[:, b, q * P:(q + 1) * P]
                        mm(o, hh, w2_h[:, b, :], start=(b == 0), stop=False)
                        mm(o, hh, w2_l[:, b, :], start=False, stop=False)
                        last = mm(o, hl, w2_h[:, b, :], start=False, stop=(b == HB - 1))
                last.then_inc(sm["z_ready"], 1)

            def ranks(p):
                pe.wait_ge(sm["hits_ready"], p + 1)
                mm(LG_PS[:, 0:E], before[:], cnt[:, 0, :], start=True, stop=True)
                mm(LG_PS[:, E:2 * E], ones[:], cnt[:, 0, :], start=True, stop=True).then_inc(sm["rank_ready"], 1)

            inputs(0)
            pe.wait_ge(sm["w_ready"], 1)
            chunk(0, True, False)
            pe.wait_ge(sm["const_ready"], 4)
            for c in range(1, NCH):
                chunk(c, c < NCH - 1, True)
                if c == PARTS[0]:
                    ranks(0)
            transposed(NCH - 1)
            logits(NCH - 1)
            ranks(1)

            def xt(g, k):
                ii = g // RING if isinstance(g, int) else None
                pe.wait_ge(xb_loaded[k % 4], 16 * (ii + 1) if ii is not None else 4 * (g - k % 4) + 16)
                wait(pe, sm["xb_lo"], g)
                pe.transpose(XTB_PS[:, 0:P], xb[:, k % 4, 0:D], ident[:]).then_inc(sm["xTb_ready"], 1)

            def expert_of(g):
                at = expert[0:1, g:g + 1] if isinstance(g, int) else expert[0:1, bass.ds(g, 1)]
                return pe.value_load(at, min_val=0, max_val=E - 1)

            def step(p, s, k, g, acts):
                if isinstance(s, int) and s == 0:
                    if p == 0:
                        pe.wait_ge(sm["r_ready"], NCH)
                        pe.wait_ge(sm["fw_lo"], NFW)
                        pe.wait_ge(sm["bias_ready"], 1)
                    pe.wait_ge(sm["route_ready"], p + 1)
                    xt(g, k)
                if acts[0]:
                    v = expert_of(g)
                    pe.wait_ge(sm["xb_lo"], g + 1)
                    wait(pe, sm["gelu_b"], g - 1)
                    o = PRE_PS[k % 2][:]
                    mm(o, sel[k % 4], bpk[:, 0:H], start=True, stop=False)
                    mm(o, xbt_h[k % 2], fw1_h[:, bass.ds(v * H, H)], start=False, stop=False)
                    mm(o, xbt_h[k % 2], fw1_l[:, bass.ds(v * H, H)], start=False, stop=False)
                    mm(o, xbt_l[k % 2], fw1_h[:, bass.ds(v * H, H)], start=False, stop=True).then_inc(sm["preb_ready"], 1)
                if acts[1]:
                    pe.wait_ge(sm["gelu_b"], g)
                    wait(pe, sm["htl_ready"], g - 2)
                    for b in range(HB):
                        last = pe.transpose(HT_PS[(k - 1) % 2][:, b * P:(b + 1) * P], hb[:, (k - 1) % 2, b * P:(b + 1) * P], ident[:])
                    last.then_inc(sm["hT_ready"], 1)
                if acts[3]:
                    xt(g + 1, k + 1)
                if acts[2]:
                    v = expert_of(g - 2)
                    pe.wait_ge(sm["htl_ready"], g - 1)
                    wait(pe, sm["yo_ready"], g - 3)
                    o = YB_PS[k % 2]
                    for b in range(HB):
                        mm(o[:, 0:2 * D], ht_h[k % 2][:, b * P:(b + 1) * P],
                           fw2[:, bass.ds(v * HB + b, 1), :].rearrange("p a n -> p (a n)"), start=(b == 0), stop=False)
                    for b in range(HB):
                        mm(o[:, 0:D], ht_l[k % 2][:, b * P:(b + 1) * P],
                           fw2[:, bass.ds(v * HB + b, 1), 0:D].rearrange("p a n -> p (a n)"), start=False, stop=False)
                    mm(o[:, 0:D], sel[(k - 2) % 4], bpk[:, H:H + D], start=False, stop=True).then_inc(sm["yb_ready"], 1)

            for p in range(2):
                walk(pe, p, slots[p], slot0[p], step)


def walk(eng, p, M, g0, step):
    def acts(s):
        return s < M, 1 <= s <= M, 2 <= s, s + 1 < M

    for s in range(RING):
        step(p, s, s, g0 + s, acts(s))
    with eng.Fori(1, M // RING - 1) as i:
        for k in range(RING):
            step(p, RING * i + k, k, RING * i + (g0 + k), (True, True, True, True))
    for s in range(M - RING, M + 2):
        step(p, s, s % RING, g0 + s, acts(s))


_INS = ["L0_attn_x3d", "L0_attn_nu_log", "L0_attn_theta_log", "L0_attn_B_re", "L0_attn_B_im", "L0_attn_C_re",
        "L0_attn_C_im", "L0_attn_D_mat", "L0_attn_W1", "L0_attn_W2", "L0_attn_res_logit",
        "L0_ffn_Wg", "L0_ffn_W1", "L0_ffn_b1", "L0_ffn_W2", "L0_ffn_b2"]
_OUTS = [((16, 256, 128), "float32")]


def kernel(**inputs):
    import numpy as _np
    import concourse.bacc as _bacc
    from concourse import mybir as _mybir
    from concourse.bass_utils import run_bass_kernel_spmd as _run

    nc = _bacc.Bacc("TRN2", target_bir_lowering=False, num_devices=1)
    arrays, args = {}, []
    for name in _INS:
        a = _np.ascontiguousarray(inputs[name])
        a = a.reshape(a.shape or (1,))
        arrays[f"in_{name}_dram"] = a
        args.append(nc.dram_tensor(f"in_{name}_dram", a.shape, _mybir.dt.from_np(a.dtype), kind="ExternalInput").ap())
    for i, (shape, dtype) in enumerate(_OUTS):
        dt = _mybir.dt.from_np(_np.dtype(dtype))
        args.append(nc.dram_tensor(f"out_{i}_dram", shape, dt, kind="ExternalOutput").ap())
    build(nc, *args)
    r = _run(nc, [arrays], core_ids=[0])
    return r.results[0]["out_0_dram"]
```

```python
from contextlib import ExitStack

import concourse.bass as bass
from concourse import mybir

P = 128
F32 = mybir.dt.float32
F32R = mybir.dt.float32r
U32 = mybir.dt.uint32
I32 = mybir.dt.int32
ALU = mybir.AluOpType
ACT = mybir.ActivationFunctionType
AX_X = mybir.AxisListType.X

D = 128
NS = 32
H = 512
HB = H // P
E = 8
CHUNK = 512
QT = CHUNK // P
ROW = D + 2
EPS = 1e-5
ROUND = 1.5 * 2.0**23
ROUND15 = 1.5 * 2.0**8
TWO_PI = 6.283185
BIG = 3.0e38
PARTS = (3, 5)
SQ = 3
SLOTS = SQ * P
YO = 21


def wait(eng, sem, value):
    if isinstance(value, int) and value <= 0:
        return
    eng.wait_ge(sem, value)


def build(nc, x, nu_log, theta_log, B_re, B_im, C_re, C_im, D_mat, W1, W2, res_logit,
          Wg, FW1, fb1, FW2, fb2, out):
    NSEQ, S, _ = x.shape
    T = NSEQ * S
    NCH = T // CHUNK
    NT = T // P
    assert sum(PARTS) == NCH
    tiles = [QT * n for n in PARTS]
    slots = [(2 * n * P + E * (SLOTS - 1)) // SLOTS for n in tiles]
    tile0 = [0, tiles[0]]
    slot0 = [0, slots[0]]
    MT = sum(slots)
    MMAX = max(slots)
    NTP = max(tiles)
    starts = [0, PARTS[0]]

    x_t = x.rearrange("b s d -> (b s) d").rearrange("(c q p) d -> c p q d", q=QT, p=P)
    out_t = out.rearrange("b s d -> (b s) d").rearrange("(c q p) d -> c p q d", q=QT, p=P)

    ctx = ExitStack()
    with ctx:
        def sb(name, shape, dt=F32):
            return ctx.enter_context(nc.sbuf_tensor(name, shape, dt))

        def sem(name):
            return ctx.enter_context(nc.semaphore(name))

        slots_d = nc.dram_tensor("slots_d", [MT * SLOTS, ROW], F32, kind="Internal").ap()
        results_d = nc.dram_tensor("results_d", [2 * T + MT * SLOTS, D], F32, kind="Internal").ap()

        bank = [ctx.enter_context(nc.psum_tensor(f"bank{i}", [P, 512], F32)) for i in range(8)]
        XT_PS, BU_PS, Y_PS, Z_PS, R_PS, LG_PS = bank[0], bank[1], bank[2], bank[5], bank[6], bank[7]
        H_PS = [bank[3], bank[4]]
        XTB_PS, ZB_PS, YB_PS = bank[0], [bank[1], bank[2]], [bank[5], bank[6]]

        ident = sb("ident", [P, P])
        ones = sb("ones", [P, P])
        before = sb("before", [P, P])
        rev = sb("rev", [P, E])
        tok = sb("tok", [P, NT])
        dump = sb("dump", [P, MT * SQ])
        jio = sb("jio", [P, MMAX])
        restart = sb("restart", [P, E * NTP])
        zeros = sb("zeros", [P, 4 * ROW])
        base_e = sb("base_e", [P, 4])
        halves = sb("halves", [P, 4])
        minus = sb("minus", [P, 4])
        epss = sb("epss", [P, 8])
        scratch = sb("scratch", [P, 1])
        mhalves = sb("mhalves", [P, 4])
        logs = sb("logs", [P, 2])
        exps = sb("exps", [P, 2])
        negnu = sb("negnu", [P, 1])
        decay = sb("decay", [P, 1])
        om = sb("om", [P, 1])
        gam = sb("gam", [P, 1])
        turn = sb("turn", [P, 4])
        late = sb("late", [P, 4 * CHUNK])
        early = sb("early", [P, 4 * P + 2 * NS + S + 2 * E])
        steps = early[:, 4 * P + 2 * NS:4 * P + 2 * NS + S]
        ph, ph2 = (late[:, n * CHUNK:(n + 1) * CHUNK].rearrange("p (a s) -> p a s", a=2) for n in range(2))
        cs = sb("cs", [P, 2, S])
        tin = sb("tin", [P, S])
        rdec = sb("rdec", [P, 2, S])
        sgl = sb("sgl", [P, 4])
        ball, dm = early[:, 0:P], early[:, P:2 * P]
        cc = early[:, 2 * P:4 * P].rearrange("p (a n) -> p a n", a=2)
        cre, cim = early[:, 4 * P:4 * P + NS], early[:, 4 * P + NS:4 * P + 2 * NS]
        bt_h, bt_l = sb("bt_h", [P, P], F32R), sb("bt_l", [P, P], F32R)
        dt_h, dt_l = sb("dt_h", [P, P], F32R), sb("dt_l", [P, P], F32R)
        wcs = sb("wcs", [P, 2, P])
        wuse = [sb(f"wuse{i}", [P, 4, H], F32R) for i in range(2)]
        w1_h, w1_l, w2_h, w2_l = (wuse[0][:, n, :] for n in range(4))
        wg = sb("wg", [P, E])
        wgc = sb("wgc", [P, E])
        fst = late[:, 2 * CHUNK:4 * CHUNK].rearrange("p (a h) -> p a h", a=2)
        fw = sb("fw", [P, E, 4 * H], F32R)
        fbias = sb("fbias", [P, E, HB + 1])
        buse = sb("buse", [P, 2, HB + 1])
        work = sb("work", [P, max(YO * SLOTS, 10 * CHUNK)])
        pt, ut, qc, qs = (work[:, n * CHUNK:(n + 1) * CHUNK] for n in range(4))
        xr = work[:, 4 * CHUNK:6 * CHUNK].rearrange("p (k q d) -> p k q d", k=2, q=QT)
        xt32 = work[:, 6 * CHUNK:8 * CHUNK].rearrange("p (k n) -> p k n", k=2)
        aw_st = work[:, 8 * CHUNK:10 * CHUNK].rearrange("p (a h) -> p a h", a=2)
        yo = work[:, 0:YO * SLOTS].rearrange("p (m q d) -> p m q d", m=YO, q=SQ)
        xt_h, xt_l = sb("xt_h", [P, 2, CHUNK], F32R), sb("xt_l", [P, 2, CHUNK], F32R)
        y_h, y_l = sb("y_h", [P, CHUNK], F32R), sb("y_l", [P, CHUNK], F32R)
        h32 = sb("h32", [P, 2, CHUNK])
        h_h, h_l = sb("h_h", [P, HB, CHUNK], F32R), sb("h_l", [P, HB, CHUNK], F32R)
        rt = sb("rt", [P, CHUNK])
        st6 = sb("st6", [P, QT, 6])
        mv = sb("mv", [P, QT, 2])
        var_e = sb("var_e", [P, QT])
        nmean = sb("nmean", [P, QT])
        rstd = sb("rstd", [P, NT])
        nmr = sb("nmr", [P, QT])
        rows = sb("rows", [P, 2, NT, ROW])
        bst = rows[0:E, 0].rearrange("p t r -> p (t r)")[:, 0:H + D]
        lg = sb("lg", [P, NT, E])
        m12 = sb("m12", [P, 2, NTP])
        s12 = sb("s12", [P, 2, NTP])
        n = NTP * E
        oh = late[:, 0:2 * n].rearrange("p (k t e) -> p k t e", k=2, e=E)
        lg2, dst = (late[:, i * n:(i + 1) * n].rearrange("p (t e) -> p t e", e=E) for i in (2, 3))
        hits, incl = (late[:, i * n:(i + 1) * n] for i in (4, 5))
        eq, sc = (early[:, i * n:(i + 1) * n].rearrange("p (t e) -> p t e", e=E) for i in range(2))
        dk = sb("dk", [P, 2, NTP])
        slot_i = sb("slot_i", [P, 2, NT], U32)
        xin, xex = (early[:, 2 * n + i * NTP * (E + 1):2 * n + (i + 1) * NTP * (E + 1)] for i in range(2))
        den = sb("den", [P, NTP])
        rden = sb("rden", [P, NTP])
        cnt = sb("cnt", [P, 8, E])
        at = 2 * n + 2 * NTP * (E + 1)
        cmp = early[:, at:at + MMAX * E].rearrange("p (m e) -> p m e", e=E)
        ej = sb("ej", [P, MMAX])
        ej7 = sb("ej7", [P, MMAX])
        expert = sb("expert", [P, MT], I32)
        ht_h = [h_h[:, b, 0:SLOTS] for b in range(HB)]
        ht_l = [h_l[:, b, 0:SLOTS] for b in range(HB)]
        xb = late[:, 2 * CHUNK:2 * CHUNK + 2 * SQ * ROW].rearrange("p (k q r) -> p k q r", k=2, q=SQ)
        xbt_h = [xt_h[:, k, 0:SLOTS] for k in range(2)]
        xbt_l = [xt_l[:, k, 0:SLOTS] for k in range(2)]
        yt = rt
        wslot = sb("wslot", [P, MT * SQ])
        dest = sb("dest", [P, MT * SQ], U32)
        sent = rows[:, 1].rearrange("p t r -> p (t r)")
        y01 = sent[:, 0:4 * CHUNK].rearrange("p (k a q d) -> p k a q d", k=2, a=2, q=QT)
        res = sent[:, 4 * CHUNK:6 * CHUNK].rearrange("p (k q d) -> p k q d", k=2, q=QT)
        r2 = sent[:, 6 * CHUNK:7 * CHUNK].rearrange("p (q d) -> p q d", q=QT)
        r3 = zeros[:, 0:CHUNK].rearrange("p (q d) -> p q d", q=QT)

        names = """zero_ready const_ready par_loaded aw_loaded
            exps_ready negnu_ready decay_ready om_ready gam_ready dve_link pool_link sig_exp cs_ready
            tables_ready ball_ready cc_ready setup_t setup_sb w_ready wgm_ready wgc_ready fw_hi fw_lo
            xT_ready xt_sb x_hi x_lo bu_ready p_ready u_ready q_ready y_ready y_hi y_lo
            pre_a h_act hh_ready hl_ready z_ready r_ready st_ready mv_ready ve_ready rstd_ready nmr_ready
            rt_ready row0_ready row1_ready lg_ready lg_sb
            hits_ready rank_ready rank_sb xin_ready xex_ready route_ready
            dispatched0 dispatched1 prefilled bias_loaded biasT_ready fbias_ready
            xTb_ready meta_ready wuse_ready xb_hi xb_lo preb_ready gelu_b hbh_ready hbh1_ready hbl_ready
            zb_ready yt_ready yT_ready yo_ready returned0 returned1
            f_sum f_r f_st f_mv f_ve f_rstd f_nmr f_res""".split()
        sm = {n: sem(n) for n in names}
        xr_loaded = [sem(f"xr_loaded{i}") for i in range(2)]
        fst_loaded = [sem(f"fst_loaded{i}") for i in range(2)]
        xb_loaded = [sem(f"xb_loaded{i}") for i in range(2)]
        y01_loaded = [sem(f"y01_loaded{i}") for i in range(2)]
        stored = [sem(f"stored{i}") for i in range(2)]

        NFW = 2 * E

        def fw_src(n):
            return FW1[n] if n < E else FW2[n - E].rearrange("(c p) d -> p c d", p=P)

        def fw_stage(n):
            return fst[:, n % 2, :]

        def fw_stage_in(n):
            return fst[:, n % 2, :] if n < E else fst[:, n % 2, :].rearrange("p (c d) -> p c d", c=HB)

        def fw_dst(n, part):
            place = 2 * (n // E) + part
            return fw[:, n % E, place * H:(place + 1) * H]

        def wait_loaded(eng, g, k):
            eng.wait_ge(xb_loaded[k], 8 * (g - k) + 16)

        block = ctx.enter_context(nc.Block())

        @block.sync
        def _(sp):
            for c in range(2):
                sp.dma_start(xr[:, c], x_t[c]).then_inc(xr_loaded[c], 16)
            for k in range(4):
                rng = slice(k * NS, (k + 1) * NS)
                sp.dma_start(logs[rng, 0:1], theta_log.rearrange("(n a) -> n a", a=1)).then_inc(sm["par_loaded"], 16)
                sp.dma_start(logs[rng, 1:2], nu_log.rearrange("(n a) -> n a", a=1)).then_inc(sm["par_loaded"], 16)
                sp.dma_start(ball[rng, :], B_re if k in (0, 3) else B_im).then_inc(sm["par_loaded"], 16)
            sp.dma_start(cre[:], C_re).then_inc(sm["par_loaded"], 16)
            sp.dma_start(cim[:], C_im).then_inc(sm["par_loaded"], 16)
            sp.dma_start(dm[:], D_mat).then_inc(sm["par_loaded"], 16)
            sp.dma_start(sgl[:, 0:1], bass.AP(tensor=res_logit.tensor, offset=0, ap=[[0, P], [1, 1]])).then_inc(sm["par_loaded"], 16)
            sp.dma_start(wg[:], Wg).then_inc(sm["par_loaded"], 16)
            sp.dma_start(aw_st[:, 0, :], W1).then_inc(sm["aw_loaded"], 16)
            sp.dma_start(aw_st[:, 1, :].rearrange("p (c d) -> p c d", c=HB),
                         W2.rearrange("(c p) d -> p c d", p=P)).then_inc(sm["aw_loaded"], 16)
            sp.wait_ge(sm["zero_ready"], 1)
            n = MT * SQ // 4
            sp.dma_start(slots_d.rearrange("(p a b) r -> p a (b r)", p=P, b=4),
                         zeros[:, :].rearrange("p (a n) -> p a n", a=1).to_broadcast([P, n, 4 * ROW])).then_inc(sm["prefilled"], 16)
            sp.dma_start(bst[:, 0:H], fb1).then_inc(sm["bias_loaded"], 16)
            sp.dma_start(bst[:, H:H + D], fb2).then_inc(sm["bias_loaded"], 16)

            def weights(n):
                wait(sp, sm["fw_lo"], n - 1)
                sp.dma_start(fw_stage_in(n), fw_src(n)).then_inc(fst_loaded[n % 2], 16)

            for n in range(2):
                weights(n)
            for c in range(NCH):
                if c + 2 < NCH:
                    sp.wait_ge(sm["xT_ready"], c + 1)
                    sp.dma_start(xr[:, c % 2], x_t[c + 2]).then_inc(xr_loaded[c % 2], 16)
                for n in range(2 * c + 2, min(2 * c + 4, NFW)):
                    weights(n)

            sp.wait_ge(sm["fw_lo"], NFW)
            for p in range(2):
                M, g0 = slots[p], slot0[p]
                sp.wait_ge(sm[f"dispatched{p}"], 16 * 2 * tiles[p])

                def load(g, k):
                    wait(sp, sm["xTb_ready"], g - 1)
                    wait(sp, sm["meta_ready"], g - 1)
                    sp.dma_start(xb[:, k], slots_d[bass.ds(g * SLOTS, SLOTS), :].rearrange("(q p) r -> p q r", p=P)).then_inc(xb_loaded[k], 16)

                load(g0, g0 % 2)
                load(g0 + 1, (g0 + 1) % 2)
                with sp.Fori(1, M // 2) as i:
                    for k in range(2):
                        load(2 * i + (g0 + k), (g0 + k) % 2)
                if M % 2:
                    load(g0 + M - 1, (g0 + M - 1) % 2)

            def results(c, k):
                for a in range(2):
                    src = results_d[bass.ds(c * CHUNK + a * T, CHUNK), :].rearrange("(q p) d -> p q d", p=P)
                    sp.dma_start(y01[:, k, a], src).then_inc(y01_loaded[k], 16)

            def store(c, k):
                sp.dma_start(out_t[c] if isinstance(c, int) else
                             out_t[bass.ds(c, 1)].rearrange("a p q d -> (a p) q d"), res[:, k]).then_inc(stored[k], 16)

            sp.wait_ge(sm["returned0"], 16 * SQ * slots[0])
            sp.wait_ge(sm["returned1"], 16 * SQ * slots[1])
            for k in range(2):
                results(k, k)
            with sp.Fori(0, NCH // 2 - 1) as i:
                for k in range(2):
                    sp.wait_ge(sm["f_res"], 2 * i + (k + 1))
                    store(2 * i + k, k)
                    results(2 * i + (k + 2), k)
            for k in range(2):
                sp.wait_ge(sm["f_res"], NCH - 1 + k)
                store(NCH - 2 + k, k)
            for k in range(2):
                sp.wait_ge(stored[k], 16 * (NCH // 2))
            sp.wait_ge(sm["prefilled"], 16)

        @block.gpsimd
        def _(pool):
            pool.memset(zeros[:], 0.0).then_inc(sm["zero_ready"], 1)
            pool.memset(ident[:], 0.0).then_inc(sm["pool_link"], 1)
            pool.memset(ones[:], 1.0).then_inc(sm["pool_link"], 1)
            pool.memset(restart[:], 1.0).then_inc(sm["pool_link"], 1)
            pool.memset(base_e[:], 2.718281828459045)
            pool.memset(halves[:], 0.5)
            pool.memset(minus[:], -1.0)
            pool.memset(epss[:, 0:4], EPS / 4)
            pool.memset(epss[:, 4:8], EPS)
            pool.memset(mhalves[:], -0.5).then_inc(sm["pool_link"], 1)
            pool.iota(steps[:], [[1, S]], base=0, channel_multiplier=0, allow_small_or_imprecise_dtypes=True).then_inc(sm["const_ready"], 1)
            pool.wait_ge(sm["par_loaded"], 16 * 17)
            pool.wait_ge(sm["pool_link"], 4)
            pool.tensor_tensor(exps[:], base_e[:, 0:2], logs[:], ALU.pow).then_inc(sm["exps_ready"], 1)
            pool.wait_ge(sm["exps_ready"], 1)
            pool.tensor_scalar(negnu[:], exps[:, 1:2], -1.0, None, ALU.mult).then_inc(sm["negnu_ready"], 1)
            pool.wait_ge(sm["negnu_ready"], 1)
            pool.tensor_tensor(decay[:], base_e[:, 0:1], negnu[:], ALU.pow).then_inc(sm["decay_ready"], 1)
            pool.wait_ge(sm["om_ready"], 1)
            pool.tensor_tensor(gam[:], om[:], halves[:, 0:1], ALU.pow).then_inc(sm["gam_ready"], 1)
            pool.affine_select(out=ident[:], in_=ident[:], compare_op=ALU.not_equal, fill=1.0, base=0,
                               pattern=[[-1, P]], channel_multiplier=1).then_inc(sm["const_ready"], 1)
            for a, b, src, sign in ((0, 0, cre, 1.0), (0, 1, cim, -1.0), (1, 0, cim, -1.0), (1, 1, cre, -1.0)):
                dstv = cc[:, a, :].rearrange("p (r b n) -> p r b n", r=2, b=2)[:, :, b, :]
                pool.tensor_scalar(dstv, src[:, :].rearrange("p (a n) -> p a n", a=1).to_broadcast([P, 2, NS]),
                                   sign, None, ALU.mult).then_inc(sm["cc_ready"], 1)
            pool.affine_select(out=before[:], in_=ones[:], compare_op=ALU.is_gt, fill=0.0, base=0,
                               pattern=[[1, P]], channel_multiplier=-1).then_inc(sm["const_ready"], 1)
            pool.iota(rev[:], [[-1, E]], base=E, channel_multiplier=0, allow_small_or_imprecise_dtypes=True)
            pool.iota(tok[:], [[P, NT]], base=0, channel_multiplier=1, allow_small_or_imprecise_dtypes=True)
            pool.iota(dump[:], [[P, MT * SQ]], base=2 * T, channel_multiplier=1, allow_small_or_imprecise_dtypes=True)
            pool.iota(jio[:], [[1, MMAX]], base=0, channel_multiplier=0, allow_small_or_imprecise_dtypes=True)
            pool.wait_ge(sm["pool_link"], 3)
            pool.memset(restart[:, :].rearrange("p (e t) -> p e t", e=E)[:, :, 0:1], 0.0).then_inc(sm["const_ready"], 1)

            def weights(n):
                pool.wait_ge(sm["fw_hi"], n + 1)
                pool.tensor_tensor(fw_dst(n, 1), fw_stage(n), fw_dst(n, 0).bitcast(F32), ALU.subtract).then_inc(sm["fw_lo"], 1)

            def norm(c):
                pool.wait_ge(sm["mv_ready"], QT * (c + 1))
                wait(pool, sm["row0_ready"], c)
                pool.tensor_tensor(var_e[:], mv[:, :, 1], epss[:, 0:4], ALU.add).then_inc(sm["ve_ready"], 1)
                pool.tensor_tensor(nmean[:], mv[:, :, 0], minus[:], ALU.mult)
                pool.wait_ge(sm["ve_ready"], c + 1)
                pool.tensor_tensor(rstd[:, QT * c:QT * (c + 1)], var_e[:], mhalves[:], ALU.pow).then_inc(sm["rstd_ready"], 1)
                pool.wait_ge(sm["rstd_ready"], c + 1)
                pool.tensor_tensor(nmr[:], nmean[:], rstd[:, QT * c:QT * (c + 1)], ALU.mult).then_inc(sm["nmr_ready"], 1)

            def dispatch(p, i):
                for k in range(2):
                    pool.indirect_dma_start(out=slots_d, out_offset=bass.IndirectOffsetOnAxis(ap=slot_i[:, k, i:i + 1], axis=0),
                                            in_=rows[:, k, i, :], in_offset=None).then_inc(sm[f"dispatched{p}"], 16)

            def send_back(p, j):
                g = slot0[p] + j
                pool.wait_ge(sm["yo_ready"], g + 1)
                for q in range(SQ):
                    pool.indirect_dma_start(out=results_d, out_offset=bass.IndirectOffsetOnAxis(ap=dest[:, SQ * g + q:SQ * g + q + 1], axis=0),
                                            in_=yo[:, g % YO, q, :], in_offset=None).then_inc(sm[f"returned{p}"], 16)

            routed = PARTS[0] + 1
            first = 0
            for c in range(NCH + 1):
                for n in range(2 * c, min(2 * c + 2, NFW)):
                    weights(n)
                if c > routed:
                    if c == routed + 1:
                        pool.wait_ge(sm["prefilled"], 16)
                        pool.wait_ge(sm["route_ready"], 1)
                        pool.wait_ge(sm["row1_ready"], PARTS[0])
                    last = tiles[0] * (c - routed) // (NCH - 1 - routed) if c < NCH else tiles[0]
                    for i in range(first, last):
                        dispatch(0, i)
                    first = last
                if c:
                    norm(c - 1)
            pool.wait_ge(sm["route_ready"], 2)
            pool.wait_ge(sm["row1_ready"], NCH)
            for i in range(tile0[1], NT):
                dispatch(1, i)
            for p in range(2):
                for j in range(slots[p]):
                    send_back(p, j)

            def final_norm(c):
                pool.wait_ge(sm["f_mv"], QT * (c + 1))
                wait(pool, sm["f_res"], c)
                pool.tensor_tensor(var_e[:], mv[:, :, 1], epss[:, 4:8], ALU.add).then_inc(sm["f_ve"], 1)
                pool.tensor_tensor(nmean[:], mv[:, :, 0], minus[:], ALU.mult)
                pool.wait_ge(sm["f_ve"], c + 1)
                pool.tensor_tensor(rstd[:, 0:QT], var_e[:], mhalves[:], ALU.pow).then_inc(sm["f_rstd"], 1)
                pool.wait_ge(sm["f_rstd"], c + 1)
                pool.tensor_tensor(nmr[:], nmean[:], rstd[:, 0:QT], ALU.mult).then_inc(sm["f_nmr"], 1)

            final_norm(0)
            with pool.Fori(1, NCH) as c:
                final_norm(c)

        @block.scalar
        def _(act):
            act.wait_ge(sm["par_loaded"], 16 * 17)
            act.activation(sgl[:, 1:2], sgl[:, 0:1], ACT.Exp, scale=-1.0).then_inc(sm["sig_exp"], 1)
            act.wait_ge(sm["tables_ready"], 1)
            act.activation(cs[:, :, :].rearrange("p a s -> p (a s)"), ph[:, :, :].rearrange("p a s -> p (a s)"),
                           ACT.Sin, scale=TWO_PI).then_inc(sm["cs_ready"], 1)
            act.preload_act_table_set("gelu_apprx_tanh_and_others")

            def weights(n):
                act.wait_ge(fst_loaded[n % 2], 16 * (n // 2 + 1))
                act.copy(fw_dst(n, 0), fw_stage(n)).then_inc(sm["fw_hi"], 1)

            def x_copy(c):
                act.wait_ge(sm["xT_ready"], c + 1)
                wait(act, sm["r_ready"], c - 1)
                act.copy(xt32[:, c % 2, :], XT_PS[:]).then_inc(sm["xt_sb"], 1)

            def rows_of(c):
                act.wait_ge(sm["nmr_ready"], c + 1)
                for q in range(QT):
                    i = QT * c + q
                    last = act.activation(rows[:, 0, i, 0:D], R_PS[:, q * D:(q + 1) * D], ACT.Identity, bias=nmr[:, q:q + 1], scale=rstd[:, i:i + 1])
                last.then_inc(sm["row0_ready"], 1)
                act.wait_ge(sm["row0_ready"], c + 1)
                act.copy(rows[:, 1, QT * c:QT * (c + 1), 0:D], rows[:, 0, QT * c:QT * (c + 1), 0:D]).then_inc(sm["row1_ready"], 1)

            def chunk(c):
                act.wait_ge(sm["y_ready"], c + 1)
                wait(act, sm["pre_a"], HB * c)
                act.copy(y_h[:], Y_PS[:]).then_inc(sm["y_hi"], 1)
                if c >= 2:
                    rows_of(c - 2)
                for b in range(HB):
                    n = HB * c + b
                    act.wait_ge(sm["pre_a"], n + 1)
                    wait(act, sm["hl_ready"], n - 1)
                    act.activation(h32[:, b % 2, :], H_PS[b % 2][:], ACT.Gelu_apprx_tanh).then_inc(sm["h_act"], 1)
                    act.wait_ge(sm["h_act"], n + 1)
                    wait(act, sm["z_ready"], c)
                    act.copy(h_h[:, b, :], h32[:, b % 2, :]).then_inc(sm["hh_ready"], 1)
                if c + 2 < NCH:
                    x_copy(c + 2)

            def softmax_exp(p):
                act.wait_ge(sm["xin_ready"], p + 1)
                n = tiles[p] * (E + 1)
                act.activation(xex[:, 0:n], xin[:, 0:n], ACT.Exp).then_inc(sm["xex_ready"], 1)

            x_copy(0)
            x_copy(1)
            for n in range(2):
                weights(n)
            for c in range(NCH):
                chunk(c)
                for n in range(2 * c + 2, min(2 * c + 4, NFW)):
                    weights(n)
                if c == PARTS[0]:
                    softmax_exp(0)
                    act.preload_act_table_set("gelu_apprx_tanh_and_others")
            rows_of(NCH - 2)
            rows_of(NCH - 1)
            softmax_exp(1)
            act.preload_act_table_set("gelu_and_others")

            def step(s, g, k, now, prev, nxt):
                if prev:
                    act.wait_ge(sm["zb_ready"], g)
                    wait(act, sm["yT_ready"], g - 1)
                    act.activation(yt[:, 0:SLOTS], ZB_PS[1 - k][:, 0:SLOTS], ACT.Identity,
                                   bias=buse[:, 1 - k, HB:HB + 1]).then_inc(sm["yt_ready"], 1)
                if now:
                    for b in range(HB):
                        act.wait_ge(sm["preb_ready"], HB * g + (b + 1))
                        wait(act, sm["hbl_ready"], HB * g + (b - 1))
                        act.activation(h32[:, b % 2, 0:SLOTS], H_PS[b % 2][:, 0:SLOTS], ACT.Gelu,
                                       bias=buse[:, k, b:b + 1]).then_inc(sm["gelu_b"], 1)
                        if b % 2 == 0:
                            act.wait_ge(sm["gelu_b"], HB * g + (b + 1))
                            wait(act, sm["zb_ready"], g)
                            act.copy(ht_h[b], h32[:, b % 2, 0:SLOTS]).then_inc(sm["hbh_ready"], 1)
                if nxt:
                    act.wait_ge(sm["xTb_ready"], g + 2)
                    wait(act, sm["preb_ready"], HB * g)
                    act.copy(xbt_h[1 - k], XTB_PS[:, 0:SLOTS]).then_inc(sm["xb_hi"], 1)
                if prev:
                    act.wait_ge(sm["yT_ready"], g)
                    act.wait_ge(sm["meta_ready"], g)
                    for q in range(SQ):
                        i = (g - 1) * SQ + q
                        w = wslot[:, i:i + 1] if isinstance(i, int) else wslot[:, bass.ds(i, 1)]
                        last = act.activation(row_of_yo(g - 1, q), YB_PS[1 - k][:, q * D:(q + 1) * D], ACT.Copy, scale=w)
                    last.then_inc(sm["yo_ready"], 1)

            def row_of_yo(g, q):
                if isinstance(g, int):
                    return yo[:, g % YO, q, :]
                return yo[:, bass.ds(g % YO, 1), q, :].rearrange("p a d -> p (a d)")

            def first_x(g, k):
                act.wait_ge(sm["xTb_ready"], g + 1)
                wait(act, sm["preb_ready"], HB * (g - 1))
                act.copy(xbt_h[k], XTB_PS[:, 0:SLOTS]).then_inc(sm["xb_hi"], 1)

            for p in range(2):
                first_x(slot0[p], slot0[p] % 2)
                cuts = {}
                if p == 1:
                    cuts = {YO - slot0[1] + 1: lambda: act.wait_ge(sm["returned0"], 16 * SQ * slots[0])}
                walk(act, slots[p], slot0[p], step, cuts)

            act.wait_ge(sm["f_r"], 1)

            def final_apply(c, k):
                act.wait_ge(sm["f_nmr"], c + 1)
                wait(act, stored[k], 8 * (c - k))
                for q in range(QT):
                    last = act.activation(res[:, k, q, :], r3[:, q, :], ACT.Identity, bias=nmr[:, q:q + 1], scale=rstd[:, q:q + 1])
                last.then_inc(sm["f_res"], 1)

            for k in range(2):
                final_apply(k, k)
            with act.Fori(1, NCH // 2) as i:
                for k in range(2):
                    final_apply(2 * i + k, k)

        @block.vector
        def _(dve):
            chain = [0]

            def link(ins):
                chain[0] += 1
                ins.then_inc(sm["dve_link"], 1)
                dve.wait_ge(sm["dve_link"], chain[0])

            dve.wait_ge(sm["exps_ready"], 1)
            link(dve.tensor_scalar(turn[:, 0:1], exps[:, 0:1], 0.15915494309189535, None, ALU.mult))
            link(dve.tensor_scalar(turn[:, 1:2], turn[:, 0:1], ROUND, -ROUND, ALU.add, ALU.add))
            link(dve.tensor_tensor(turn[:, 0:1], turn[:, 0:1], turn[:, 1:2], ALU.subtract))
            link(dve.tensor_scalar(turn[:, 2:3], turn[:, 0:1], ROUND15, -ROUND15, ALU.add, ALU.add))
            link(dve.tensor_tensor(turn[:, 3:4], turn[:, 0:1], turn[:, 2:3], ALU.subtract))
            dve.wait_ge(sm["const_ready"], 1)
            link(dve.tensor_scalar(ph[:, 0, :], steps[:], turn[:, 2:3], None, ALU.mult))
            link(dve.tensor_scalar(ph2[:, 0, :], ph[:, 0, :], ROUND, -ROUND, ALU.add, ALU.add))
            link(dve.tensor_tensor(ph[:, 1, :], ph[:, 0, :], ph2[:, 0, :], ALU.subtract))
            link(dve.scalar_tensor_tensor(out=ph2[:, 1, :], in0=steps[:], scalar=turn[:, 3:4], in1=ph[:, 1, :], op0=ALU.mult, op1=ALU.add))
            dve.tensor_scalar(ph2[:, 0, :], ph2[:, 1, :], 0.25, None, ALU.add)
            dve.wait_ge(sm["decay_ready"], 1)
            link(dve.tensor_tensor(om[:], decay[:], decay[:], ALU.mult))
            dve.tensor_scalar(om[:], om[:], -1.0, 1.0, ALU.mult, ALU.add).then_inc(sm["om_ready"], 1)
            link(dve.tensor_scalar(cs[:, :, :], ph2[:, :, :], ROUND, -ROUND, ALU.add, ALU.add))
            dve.tensor_tensor(ph[:, :, :], ph2[:, :, :], cs[:, :, :], ALU.subtract).then_inc(sm["tables_ready"], 1)
            link(dve.tensor_scalar(rdec[:, :, :], ph2[:, :, :], 0.0, decay[:, 0:1], ALU.mult, ALU.add))
            link(dve.memset(rdec[:, :, 0:1], 0.0))
            dve.wait_ge(sm["gam_ready"], 1)
            link(dve.tensor_scalar(ball[:], ball[:], gam[:, 0:1], None, ALU.mult))
            dve.tensor_scalar(ball[96:P, :], ball[96:P, :], -1.0, None, ALU.mult).then_inc(sm["ball_ready"], 1)
            dve.wait_ge(sm["aw_loaded"], 32)
            dve.tensor_copy(w1_h, aw_st[:, 0, :])
            link(dve.tensor_copy(w2_h, aw_st[:, 1, :]))
            dve.tensor_tensor(w1_l, aw_st[:, 0, :], w1_h.bitcast(F32), ALU.subtract)
            dve.tensor_tensor(w2_l, aw_st[:, 1, :], w2_h.bitcast(F32), ALU.subtract).then_inc(sm["w_ready"], 1)
            dve.wait_ge(sm["sig_exp"], 1)
            link(dve.tensor_scalar(sgl[:, 2:3], sgl[:, 1:2], 1.0, None, ALU.add))
            link(dve.reciprocal(sgl[:, 3:4], sgl[:, 2:3]))
            link(dve.tensor_scalar(sgl[:, 2:3], sgl[:, 3:4], 0.5, None, ALU.mult))
            dve.wait_ge(sm["setup_t"], 1)
            dve.tensor_copy(bt_h[:], Z_PS[:, 0:P])
            dve.tensor_copy(dt_h[:], Z_PS[:, P:2 * P])
            link(dve.tensor_copy(wcs[:, :, :].rearrange("p a n -> p (a n)"), Z_PS[:, 2 * P:4 * P]))
            dve.tensor_tensor(bt_l[:], Z_PS[:, 0:P], bt_h[:].bitcast(F32), ALU.subtract)
            dve.tensor_tensor(dt_l[:], Z_PS[:, P:2 * P], dt_h[:].bitcast(F32), ALU.subtract).then_inc(sm["setup_sb"], 1)
            dve.wait_ge(sm["wgm_ready"], 1)
            dve.scalar_tensor_tensor(out=wgc[:], in0=LG_PS[:, 0:E], scalar=-1.0 / D, in1=wg[:], op0=ALU.mult, op1=ALU.add).then_inc(sm["wgc_ready"], 1)
            dve.wait_ge(sm["biasT_ready"], 1)
            dve.tensor_copy(fbias[:, :, :].rearrange("p e b -> p b e"), H_PS[0][:, 0:E * (HB + 1)].rearrange("p (b e) -> p b e", e=E)).then_inc(sm["fbias_ready"], 1)
            dve.wait_ge(sm["cs_ready"], 1)
            dve.tensor_copy(tin[0:64, :], cs[0:64, 0, :])
            link(dve.tensor_copy(tin[64:P, :], cs[64:P, 1, :]))

            def both(t):
                return t.rearrange("p (a s) -> p a s", a=1).to_broadcast([P, 2, S])

            def two(t):
                return t.rearrange("p (a s) -> p a s", a=2)

            def x_split(c):
                dve.wait_ge(sm["xt_sb"], c + 1)
                wait(dve, sm["y_ready"], c - 1)
                dve.tensor_copy(xt_h[:, c % 2, :], xt32[:, c % 2, :]).then_inc(sm["x_hi"], 1)
                dve.wait_ge(sm["x_hi"], c + 1)
                dve.tensor_tensor(xt_l[:, c % 2, :], xt32[:, c % 2, :], xt_h[:, c % 2, :].bitcast(F32), ALU.subtract).then_inc(sm["x_lo"], 1)

            def turn_in(c):
                dve.wait_ge(sm["bu_ready"], c + 1)
                dve.tensor_tensor(two(pt), two(BU_PS[:, :]), both(tin[:, :]), ALU.mult).then_inc(sm["p_ready"], 1)
                dve.wait_ge(sm["p_ready"], c + 1)
                dve.tensor_tensor_scan(ut, rdec[:, :, :].rearrange("p a s -> p (a s)"), pt, 0.0, ALU.mult, ALU.add).then_inc(sm["u_ready"], 1)

            def turn_back(c, n):
                dve.wait_ge(sm["u_ready"], c + 1)
                wait(dve, sm["y_ready"], c)
                dve.tensor_tensor(two((qc, qs)[n]), two(ut), both(cs[:, n, :]), ALU.mult).then_inc(sm["q_ready"], 1)

            def hidden_low(c, b):
                dve.wait_ge(sm["hh_ready"], HB * c + b + 1)
                dve.tensor_tensor(h_l[:, b, :], h32[:, b % 2, :], h_h[:, b, :].bitcast(F32), ALU.subtract).then_inc(sm["hl_ready"], 1)

            def stats(c):
                dve.wait_ge(sm["rt_ready"], c + 1)
                for q in range(QT):
                    dve.bn_stats(st6[:, q, :], R_PS[:, q * D:(q + 1) * D]).then_inc(sm["st_ready"], 1)

            def aggregate(c):
                dve.wait_ge(sm["st_ready"], QT * (c + 1))
                wait(dve, sm["nmr_ready"], c)
                for q in range(QT):
                    dve.bn_aggr(mv[:, q, :], st6[:, q, :]).then_inc(sm["mv_ready"], 1)

            def logits(c):
                dve.wait_ge(sm["lg_ready"], c + 1)
                dve.tensor_copy(lg[:, QT * c:QT * (c + 1), :].rearrange("p q e -> p (q e)"), LG_PS[:, 0:QT * E]).then_inc(sm["lg_sb"], 1)

            def chunk(c):
                dve.wait_ge(sm["y_hi"], c + 1)
                dve.tensor_tensor(y_l[:], Y_PS[:], y_h[:].bitcast(F32), ALU.subtract).then_inc(sm["y_lo"], 1)
                if c + 1 < NCH:
                    turn_in(c + 1)
                    turn_back(c + 1, 0)
                hidden_low(c, 0)
                if c + 1 < NCH:
                    turn_back(c + 1, 1)
                for b in range(1, HB):
                    hidden_low(c, b)
                if c >= 1:
                    stats(c - 1)
                    logits(c - 1)
                dve.wait_ge(sm["z_ready"], c + 1)
                wait(dve, sm["rt_ready"], c)
                dve.scalar_tensor_tensor(out=rt[:], in0=Z_PS[:], scalar=sgl[:, 2:3], in1=xt32[:, c % 2, :],
                                         op0=ALU.mult, op1=ALU.add).then_inc(sm["r_ready"], 1)
                if c >= 1:
                    aggregate(c - 1)
                if c + 2 < NCH:
                    x_split(c + 2)

            def route(p):
                n, t0, M, g0 = tiles[p], tile0[p], slots[p], slot0[p]
                lgp = lg[:, t0:t0 + n, :]
                dve.wait_ge(sm["lg_sb"], starts[p] + PARTS[p])
                dve.wait_ge(sm["rstd_ready"], starts[p] + PARTS[p])

                def over_e(t):
                    return t.rearrange("p (n a) -> p n a", a=1).to_broadcast([P, n, E])

                link(dve.tensor_tensor(lgp, lgp, over_e(rstd[:, t0:t0 + n]), ALU.mult))
                for k in range(2):
                    src = lgp if k == 0 else lg2[:, 0:n, :]
                    link(dve.tensor_reduce(m12[:, k, 0:n], src, AX_X, ALU.max))
                    link(dve.tensor_tensor(eq[:, 0:n, :], src, over_e(m12[:, k, 0:n]), ALU.is_equal))
                    link(dve.tensor_tensor(sc[:, 0:n, :], eq[:, 0:n, :], rev[:, :].rearrange("p (a e) -> p a e", a=1).to_broadcast([P, n, E]), ALU.mult))
                    link(dve.tensor_reduce(s12[:, k, 0:n], sc[:, 0:n, :], AX_X, ALU.max))
                    link(dve.tensor_tensor(oh[:, k, 0:n, :], sc[:, 0:n, :], over_e(s12[:, k, 0:n]), ALU.is_equal))
                    if k == 0:
                        link(dve.scalar_tensor_tensor(out=lg2[:, 0:n, :], in0=oh[:, 0, 0:n, :], scalar=-BIG, in1=lgp, op0=ALU.mult, op1=ALU.add))
                hv = hits[:, 0:E * n]
                iv = incl[:, 0:E * n]
                link(dve.tensor_tensor(hv.rearrange("p (e t) -> p t e", e=E), oh[:, 0, 0:n, :], oh[:, 1, 0:n, :], ALU.add))
                if n != NTP:
                    rs = restart[:, :].rearrange("p (e t) -> p e t", e=E)[:, :, 0:n]
                    link(dve.tensor_copy(cmp[:, :, :].rearrange("p a b -> p (a b)")[:, 0:E * n].rearrange("p (e t) -> p e t", e=E), rs))
                    rsv = cmp[:, :, :].rearrange("p a b -> p (a b)")[:, 0:E * n]
                else:
                    rsv = restart[:]
                link(dve.tensor_tensor_scan(iv, rsv, hv, 0.0, ALU.mult, ALU.add))
                dve.tensor_copy(cnt[:, 0, :], iv.rearrange("p (e t) -> p e t", e=E)[:, :, n - 1]).then_inc(sm["hits_ready"], 1)
                dve.tensor_tensor(xin[:, 0:n * E].rearrange("p (n e) -> p n e", e=E), lgp, over_e(m12[:, 0, 0:n]), ALU.subtract)
                dve.tensor_tensor(xin[:, n * E:n * (E + 1)], m12[:, 1, 0:n], m12[:, 0, 0:n], ALU.subtract).then_inc(sm["xin_ready"], 1)
                dve.wait_ge(sm["rank_ready"], p + 1)
                dve.tensor_copy(cnt[:, 6:8, :].rearrange("p a e -> p (a e)"), LG_PS[:, 0:2 * E]).then_inc(sm["rank_sb"], 1)
                dve.wait_ge(sm["rank_sb"], p + 1)
                link(dve.tensor_scalar(cnt[:, 1, :], cnt[:, 7, :], 1.0 / SLOTS, (SLOTS - 1) / 2 / SLOTS, ALU.mult, ALU.add))
                link(dve.tensor_scalar(cnt[:, 2, :], cnt[:, 1, :], ROUND, -ROUND, ALU.add, ALU.add))
                link(dve.tensor_tensor_scan(cnt[:, 3, :], ones[:, 0:E], cnt[:, 2, :], 0.0, ALU.mult, ALU.add))
                link(dve.tensor_tensor(cnt[:, 4, :], cnt[:, 3, :], cnt[:, 2, :], ALU.subtract))
                link(dve.scalar_tensor_tensor(out=cnt[:, 5, :], in0=cnt[:, 4, :], scalar=float(SLOTS), in1=cnt[:, 6, :], op0=ALU.mult, op1=ALU.add))
                link(dve.tensor_tensor(dst[:, 0:n, :], iv.rearrange("p (e t) -> p t e", e=E),
                                       cnt[:, 5:6, :].to_broadcast([P, n, E]), ALU.add))
                off = g0 * SLOTS - 1
                for k in range(2):
                    link(dve.tensor_tensor(sc[:, 0:n, :], oh[:, k, 0:n, :], dst[:, 0:n, :], ALU.mult))
                    link(dve.tensor_reduce(dk[:, k, 0:n], sc[:, 0:n, :], AX_X, ALU.add))
                    dve.tensor_scalar(slot_i[:, k, t0:t0 + n], dk[:, k, 0:n], float(off), None, ALU.add)
                    link(dve.scalar_tensor_tensor(out=s12[:, k, 0:n], in0=dk[:, k, 0:n], scalar=-1.0, in1=tok[:, t0:t0 + n], op0=ALU.mult, op1=ALU.add))
                    dve.tensor_scalar(rows[:, k, t0:t0 + n, D], s12[:, k, 0:n], float(k * T - 2 * T - off), None, ALU.add)
                dve.wait_ge(sm["xex_ready"], p + 1)
                link(dve.tensor_reduce(den[:, 0:n], xex[:, 0:n * E].rearrange("p (n e) -> p n e", e=E), AX_X, ALU.add))
                link(dve.reciprocal(rden[:, 0:n], den[:, 0:n]))
                dve.tensor_copy(rows[:, 0, t0:t0 + n, D + 1], rden[:, 0:n])
                link(dve.tensor_tensor(rows[:, 1, t0:t0 + n, D + 1], xex[:, n * E:n * (E + 1)], rden[:, 0:n], ALU.mult))
                link(dve.tensor_tensor(cmp[:, 0:M, :], jio[:, 0:M].rearrange("p (m a) -> p m a", a=1).to_broadcast([P, M, E]),
                                       cnt[:, 3:4, :].to_broadcast([P, M, E]), ALU.is_ge))
                link(dve.tensor_reduce(ej[:, 0:M], cmp[:, 0:M, :], AX_X, ALU.add))
                link(dve.tensor_scalar(ej7[:, 0:M], ej[:, 0:M], float(E - 1), None, ALU.min))
                dve.tensor_copy(expert[:, g0:g0 + M], ej7[:, 0:M]).then_inc(sm["route_ready"], 1)

            x_split(0)
            turn_in(0)
            turn_back(0, 0)
            turn_back(0, 1)
            x_split(1)
            dve.wait_ge(sm["const_ready"], 4)
            for c in range(NCH):
                chunk(c)
                if c == PARTS[0]:
                    route(0)
            stats(NCH - 1)
            logits(NCH - 1)
            aggregate(NCH - 1)
            route(1)

            def weights_of(g, k):
                at = expert[0:1, g:g + 1] if isinstance(g, int) else expert[0:1, bass.ds(g, 1)]
                e = dve.value_load(at, min_val=0, max_val=E - 1)
                wait(dve, sm["zb_ready"], g - 1)
                dve.tensor_copy(wuse[k][:, :, :].rearrange("p a h -> p (a h)"), fw[:, bass.ds(e, 1), :].rearrange("p a h -> p (a h)"))
                wait(dve, sm["yt_ready"], g - 1)
                dve.tensor_copy(buse[:, k, :], fbias[:, bass.ds(e, 1), :].rearrange("p a b -> p (a b)")).then_inc(sm["wuse_ready"], 1)

            def meta(g, k):
                i = SQ * g
                cut = (lambda t: t[:, i:i + SQ]) if isinstance(g, int) else (lambda t: t[:, bass.ds(i, SQ)])
                wait_loaded(dve, g, k)
                dve.tensor_tensor(cut(dest), xb[:, k, :, D], cut(dump), ALU.add)
                dve.tensor_copy(cut(wslot), xb[:, k, :, D + 1]).then_inc(sm["meta_ready"], 1)

            def x_low(g, k):
                dve.wait_ge(sm["xb_hi"], g + 1)
                dve.tensor_tensor(xbt_l[k], XTB_PS[:, 0:SLOTS], xbt_h[k].bitcast(F32), ALU.subtract).then_inc(sm["xb_lo"], 1)

            def step(s, g, k, now, prev, nxt):
                if nxt:
                    weights_of(g + 1, 1 - k)
                    meta(g + 1, 1 - k)
                if now:
                    for b in range(HB):
                        if b % 2:
                            dve.wait_ge(sm["gelu_b"], HB * g + (b + 1))
                            wait(dve, sm["zb_ready"], g)
                            dve.tensor_copy(ht_h[b], h32[:, b % 2, 0:SLOTS]).then_inc(sm["hbh1_ready"], 1)
                            dve.wait_ge(sm["hbh1_ready"], 2 * g + (b // 2 + 1))
                        else:
                            dve.wait_ge(sm["hbh_ready"], 2 * g + (b // 2 + 1))
                        dve.tensor_tensor(ht_l[b], h32[:, b % 2, 0:SLOTS], ht_h[b].bitcast(F32), ALU.subtract).then_inc(sm["hbl_ready"], 1)
                if nxt:
                    x_low(g + 1, 1 - k)

            for p in range(2):
                weights_of(slot0[p], slot0[p] % 2)
                meta(slot0[p], slot0[p] % 2)
                x_low(slot0[p], slot0[p] % 2)
                walk(dve, slots[p], slot0[p], step, {})

            def final(c, k):
                dve.wait_ge(y01_loaded[k], 16 * (c - k) + 32)
                wait(dve, sm["f_st"], QT * c)
                dve.tensor_tensor(r2[:, :, :], y01[:, k, 0], y01[:, k, 1], ALU.add).then_inc(sm["f_sum"], 1)
                dve.wait_ge(sm["f_sum"], c + 1)
                wait(dve, sm["f_res"], c)
                dve.tensor_tensor(r3[:, :, :], r2[:, :, :], rows[:, 0, bass.ds(QT * c, QT), 0:D], ALU.add).then_inc(sm["f_r"], 1)
                dve.wait_ge(sm["f_r"], c + 1)
                for q in range(QT):
                    dve.bn_stats(st6[:, q, :], r3[:, q, :]).then_inc(sm["f_st"], 1)
                dve.wait_ge(sm["f_st"], QT * c + QT)
                dve.memset(scratch[:], 0.0)
                for q in range(QT):
                    dve.bn_aggr(mv[:, q, :], st6[:, q, :]).then_inc(sm["f_mv"], 1)

            for k in range(2):
                final(k, k)
            with dve.Fori(1, NCH // 2) as i:
                for k in range(2):
                    final(2 * i + k, k)

        @block.tensor
        def _(pe):
            mm = pe.matmul
            pe.wait_ge(sm["const_ready"], 2)
            pe.wait_ge(sm["ball_ready"], 1)
            pe.wait_ge(sm["cc_ready"], 4)
            pe.transpose(Z_PS[:, 0:P], ball[:], ident[:])
            pe.transpose(Z_PS[:, P:2 * P], dm[:], ident[:])
            pe.transpose(Z_PS[:, 2 * P:3 * P], cc[:, 0, :], ident[:])
            pe.transpose(Z_PS[:, 3 * P:4 * P], cc[:, 1, :], ident[:]).then_inc(sm["setup_t"], 1)
            mm(LG_PS[:, 0:E], ones[:], wg[:], start=True, stop=True).then_inc(sm["wgm_ready"], 1)
            pe.wait_ge(sm["bias_loaded"], 32)
            for b in range(HB + 1):
                last = pe.transpose(H_PS[0][:, b * E:(b + 1) * E], bst[:, b * P:(b + 1) * P], ident[0:E, 0:E])
            last.then_inc(sm["biasT_ready"], 1)

            def products(out_, wh, wl, xh, xl, start, stop):
                mm(out_, wh, xh, start=start, stop=False)
                mm(out_, wh, xl, start=False, stop=False)
                return mm(out_, wl, xh, start=False, stop=stop)

            def x_transposed(c):
                pe.wait_ge(xr_loaded[c % 2], 16 * (c // 2 + 1))
                wait(pe, sm["xt_sb"], c)
                for q in range(QT):
                    last = pe.transpose(XT_PS[:, q * P:(q + 1) * P], xr[:, c % 2, q, :], ident[:])
                last.then_inc(sm["xT_ready"], 1)

            def inputs(c):
                pe.wait_ge(sm["x_lo"], c + 1)
                wait(pe, sm["p_ready"], c)
                products(BU_PS[:], bt_h[:], bt_l[:], xt_h[:, c % 2, :], xt_l[:, c % 2, :], True, True).then_inc(sm["bu_ready"], 1)

            def logits(c):
                pe.wait_ge(sm["r_ready"], c + 1)
                wait(pe, sm["lg_sb"], c)
                if c == PARTS[0]:
                    pe.wait_ge(sm["rank_sb"], 1)
                for q in range(QT):
                    last = mm(LG_PS[:, q * E:(q + 1) * E], rt[:, q * P:(q + 1) * P], wgc[:], start=True, stop=True)
                last.then_inc(sm["lg_ready"], 1)

            def r_transposed(c):
                wait(pe, sm["row0_ready"], c)
                for q in range(QT):
                    last = pe.transpose(R_PS[:, q * D:(q + 1) * D], rt[:, q * P:(q + 1) * P], ident[:])
                last.then_inc(sm["rt_ready"], 1)

            def chunk(c):
                wait(pe, sm["y_lo"], c)
                pe.wait_ge(sm["q_ready"], 2 * c + 2)
                mm(Y_PS[:], wcs[:, 0, :], qc, start=True, stop=False)
                mm(Y_PS[:], wcs[:, 1, :], qs, start=False, stop=False)
                products(Y_PS[:], dt_h[:], dt_l[:], xt_h[:, c % 2, :], xt_l[:, c % 2, :], False, True).then_inc(sm["y_ready"], 1)
                if c + 1 < NCH:
                    inputs(c + 1)
                if c >= 1:
                    logits(c - 1)
                    r_transposed(c - 1)
                pe.wait_ge(sm["y_lo"], c + 1)
                for b in range(HB):
                    wait(pe, sm["h_act"], HB * c + b - 1)
                    products(H_PS[b % 2][:], w1_h[:, b * P:(b + 1) * P], w1_l[:, b * P:(b + 1) * P], y_h[:], y_l[:],
                             True, True).then_inc(sm["pre_a"], 1)
                if c == PARTS[0] + 1:
                    pass
                if c + 2 < NCH:
                    x_transposed(c + 2)
                wait(pe, sm["r_ready"], c)
                for b in range(HB):
                    pe.wait_ge(sm["hl_ready"], HB * c + b + 1)
                    last = products(Z_PS[:], w2_h[:, b * D:(b + 1) * D], w2_l[:, b * D:(b + 1) * D], h_h[:, b, :], h_l[:, b, :],
                                    b == 0, b == HB - 1)
                last.then_inc(sm["z_ready"], 1)

            def ranks(p):
                pe.wait_ge(sm["hits_ready"], p + 1)
                mm(LG_PS[:, 0:E], before[:], cnt[:, 0, :], start=True, stop=True)
                mm(LG_PS[:, E:2 * E], ones[:], cnt[:, 0, :], start=True, stop=True).then_inc(sm["rank_ready"], 1)

            x_transposed(0)
            x_transposed(1)
            pe.wait_ge(sm["setup_sb"], 1)
            inputs(0)
            pe.wait_ge(sm["w_ready"], 1)
            pe.wait_ge(sm["wgc_ready"], 1)
            pe.wait_ge(sm["fbias_ready"], 1)
            for c in range(NCH):
                chunk(c)
                if c == PARTS[0]:
                    pe.wait_ge(sm["const_ready"], 4)
                    ranks(0)
            pe.wait_ge(sm["r_ready"], NCH)
            logits(NCH - 1)
            r_transposed(NCH - 1)
            ranks(1)

            def xt(g, k):
                wait_loaded(pe, g, k)
                wait(pe, sm["xb_lo"], g)
                for q in range(SQ):
                    last = pe.transpose(XTB_PS[:, q * P:(q + 1) * P], xb[:, k, q, 0:D], ident[:])
                last.then_inc(sm["xTb_ready"], 1)

            def step(s, g, k, now, prev, nxt):
                w1h, w1l, w2h, w2l = (wuse[k][:, n, :] for n in range(4))
                if now:
                    pe.wait_ge(sm["wuse_ready"], g + 1)
                    pe.wait_ge(sm["xb_lo"], g + 1)
                    for b in range(HB):
                        wait(pe, sm["gelu_b"], HB * g + (b - 1))
                        products(H_PS[b % 2][:, 0:SLOTS], w1h[:, b * P:(b + 1) * P], w1l[:, b * P:(b + 1) * P],
                                 xbt_h[k], xbt_l[k], True, True).then_inc(sm["preb_ready"], 1)
                if nxt:
                    xt(g + 1, 1 - k)
                if prev:
                    pe.wait_ge(sm["yt_ready"], g)
                    wait(pe, sm["yo_ready"], g - 2)
                    for q in range(SQ):
                        last = pe.transpose(YB_PS[1 - k][:, q * D:(q + 1) * D], yt[:, q * P:(q + 1) * P], ident[:])
                    last.then_inc(sm["yT_ready"], 1)
                if now:
                    for b in range(HB):
                        pe.wait_ge(sm["hbl_ready"], HB * g + (b + 1))
                        last = products(ZB_PS[k][:, 0:SLOTS], w2h[:, b * D:(b + 1) * D], w2l[:, b * D:(b + 1) * D],
                                        ht_h[b], ht_l[b], b == 0, b == HB - 1)
                    last.then_inc(sm["zb_ready"], 1)

            pe.wait_ge(sm["row0_ready"], NCH)
            pe.wait_ge(sm["fw_lo"], NFW)
            for p in range(2):
                pe.wait_ge(sm["route_ready"], p + 1)
                xt(slot0[p], slot0[p] % 2)
                walk(pe, slots[p], slot0[p], step, {})


def walk(eng, M, g0, step, cuts):
    def one(s):
        step(s, g0 + s, (g0 + s) % 2, s < M, s >= 1, s + 1 < M)

    first = max(1, 3 - g0)
    at = [first] + sorted(cuts) + [M - 1]
    for s in range(first):
        one(s)
    for a, b in zip(at, at[1:]):
        if a in cuts:
            cuts[a]()
        if b - a >= 2:
            with eng.Fori(0, (b - a) // 2) as i:
                for k in range(2):
                    step(2 * i + (a + k), 2 * i + (g0 + a + k), (g0 + a + k) % 2, True, True, True)
        if (b - a) % 2:
            one(b - 1)
    one(M - 1)
    one(M)


_INS = ["L0_attn_x3d", "L0_attn_nu_log", "L0_attn_theta_log", "L0_attn_B_re", "L0_attn_B_im", "L0_attn_C_re",
        "L0_attn_C_im", "L0_attn_D_mat", "L0_attn_W1", "L0_attn_W2", "L0_attn_res_logit",
        "L0_ffn_Wg", "L0_ffn_W1", "L0_ffn_b1", "L0_ffn_W2", "L0_ffn_b2"]
_OUTS = [((16, 256, 128), "float32")]


def kernel(**inputs):
    import numpy as _np
    import concourse.bacc as _bacc
    from concourse import mybir as _mybir
    from concourse.bass_utils import run_bass_kernel_spmd as _run

    nc = _bacc.Bacc("TRN2", target_bir_lowering=False, num_devices=1)
    arrays, args = {}, []
    for name in _INS:
        a = _np.ascontiguousarray(inputs[name])
        a = a.reshape(a.shape or (1,))
        arrays[f"in_{name}_dram"] = a
        args.append(nc.dram_tensor(f"in_{name}_dram", a.shape, _mybir.dt.from_np(a.dtype), kind="ExternalInput").ap())
    for i, (shape, dtype) in enumerate(_OUTS):
        dt = _mybir.dt.from_np(_np.dtype(dtype))
        args.append(nc.dram_tensor(f"out_{i}_dram", shape, dt, kind="ExternalOutput").ap())
    build(nc, *args)
    r = _run(nc, [arrays], core_ids=[0])
    return r.results[0]["out_0_dram"]
```

```python
from contextlib import ExitStack

import concourse.bass as bass
from concourse import mybir

P = 128
F32 = mybir.dt.float32
F32R = mybir.dt.float32r
U32 = mybir.dt.uint32
I32 = mybir.dt.int32
ALU = mybir.AluOpType
ACT = mybir.ActivationFunctionType
AX_X = mybir.AxisListType.X

D = 128
NS = 32
H = 512
HB = H // P
E = 8
CHUNK = 512
QT = CHUNK // P
ROW = D + 2
EPS = 1e-5
ROUND = 1.5 * 2.0**23
ROUND15 = 1.5 * 2.0**8
TWO_PI = 6.283185
BIG = 3.0e38
PARTS = (3, 5)
SQ = 3
SLOTS = SQ * P
ROUTE1 = 1
PIECES = (0, 6, 10, 13, 16)
PADS = 6
FB = 4
YO = 21


def wait(eng, sem, value):
    if isinstance(value, int) and value <= 0:
        return
    eng.wait_ge(sem, value)


def build(nc, x, nu_log, theta_log, B_re, B_im, C_re, C_im, D_mat, W1, W2, res_logit,
          Wg, FW1, fb1, FW2, fb2, out):
    NSEQ, S, _ = x.shape
    T = NSEQ * S
    NCH = T // CHUNK
    NT = T // P
    assert sum(PARTS) == NCH
    tiles = [QT * n for n in PARTS]
    slots = [(2 * n * P + E * (SLOTS - 1)) // SLOTS for n in tiles]
    tile0 = [0, tiles[0]]
    slot0 = [0, slots[0]]
    MT = sum(slots)
    MMAX = max(slots)
    NTP = max(tiles)
    starts = [0, PARTS[0]]

    x_t = x.rearrange("b s d -> (b s) d").rearrange("(c q p) d -> c p q d", q=QT, p=P)
    out_t = out.rearrange("b s d -> (b s) d").rearrange("(c q p) d -> c p q d", q=QT, p=P)

    ctx = ExitStack()
    with ctx:
        def sb(name, shape, dt=F32):
            return ctx.enter_context(nc.sbuf_tensor(name, shape, dt))

        def sem(name):
            return ctx.enter_context(nc.semaphore(name))

        slots_d = nc.dram_tensor("slots_d", [MT * SLOTS, ROW], F32, kind="Internal").ap()
        results_d = nc.dram_tensor("results_d", [2 * T + MT * SLOTS, D], F32, kind="Internal").ap()

        bank = [ctx.enter_context(nc.psum_tensor(f"bank{i}", [P, 512], F32)) for i in range(8)]
        XT_PS, BU_PS, Y_PS, Z_PS, R_PS, LG_PS = bank[0], bank[1], bank[2], bank[5], bank[6], bank[7]
        H_PS = [bank[3], bank[4]]
        XTB_PS, ZB_PS, YB_PS = bank[0], [bank[1], bank[2]], [bank[5], bank[6]]

        ident = sb("ident", [P, P])
        ones = sb("ones", [P, P])
        before = sb("before", [P, P])
        rev = sb("rev", [P, E])
        tok = sb("tok", [P, NT])
        dump = sb("dump", [P, MT * SQ])
        jio = sb("jio", [P, MMAX])
        restart = sb("restart", [P, E * NTP])
        zeros = sb("zeros", [P, 4 * ROW])
        base_e = sb("base_e", [P, 4])
        halves = sb("halves", [P, 4])
        minus = sb("minus", [P, 4])
        epss = sb("epss", [P, 8])
        mhalves = sb("mhalves", [P, 4])
        logs = sb("logs", [P, 4])
        exps = sb("exps", [P, 4])
        negnu = sb("negnu", [P, 1])
        decay = sb("decay", [P, 1])
        om = sb("om", [P, 1])
        gam = sb("gam", [P, 1])
        turn = sb("turn", [P, 4])
        late = sb("late", [P, 4 * CHUNK])
        early = sb("early", [P, max(4 * P + 2 * NS + S, 2 * NTP * (2 * E + 1) + MMAX * E)])
        steps = early[:, 4 * P + 2 * NS:4 * P + 2 * NS + S]
        ph, ph2 = (late[:, n * CHUNK:(n + 1) * CHUNK].rearrange("p (a s) -> p a s", a=2) for n in range(2))
        cs = sb("cs", [P, 2, S])
        tin = sb("tin", [P, S])
        rdec = sb("rdec", [P, 2, S])
        sgl = sb("sgl", [P, 4])
        ball, dm = early[:, 0:P], early[:, P:2 * P]
        cc = early[:, 2 * P:4 * P].rearrange("p (a n) -> p a n", a=2)
        cre, cim = early[:, 4 * P:4 * P + NS], early[:, 4 * P + NS:4 * P + 2 * NS]
        bt_h, bt_l = sb("bt_h", [P, P], F32R), sb("bt_l", [P, P], F32R)
        dt_h, dt_l = sb("dt_h", [P, P], F32R), sb("dt_l", [P, P], F32R)
        wcs = sb("wcs", [P, 2, P])
        wuse = [sb(f"wuse{i}", [P, 4, H], F32R) for i in range(2)]
        w1_h, w1_l, w2_h, w2_l = (wuse[1][:, n, :] for n in range(4))
        wg = sb("wg", [P, E])
        wgc = sb("wgc", [P, E])
        fst = late[:, 2 * CHUNK:4 * CHUNK].rearrange("p (a h) -> p a h", a=2)
        fw = sb("fw", [P, E, 4 * H], F32R)
        fbias = sb("fbias", [P, E, HB + 1])
        buse = sb("buse", [P, 2, HB + 1])
        work = sb("work", [P, max(YO * SLOTS, 11 * CHUNK)])
        pt, ut, qc, qs = (work[:, n * CHUNK:(n + 1) * CHUNK] for n in range(4))
        xr = work[:, 4 * CHUNK:6 * CHUNK].rearrange("p (k q d) -> p k q d", k=2, q=QT)
        xt32 = work[:, 6 * CHUNK:9 * CHUNK].rearrange("p (k n) -> p k n", k=3)
        aw_st = work[:, 9 * CHUNK:11 * CHUNK].rearrange("p (a h) -> p a h", a=2)
        yo = work[:, 0:YO * SLOTS].rearrange("p (m q d) -> p m q d", m=YO, q=SQ)
        xt_h, xt_l = sb("xt_h", [P, 2, CHUNK], F32R), sb("xt_l", [P, 2, CHUNK], F32R)
        y_h, y_l = sb("y_h", [P, CHUNK], F32R), sb("y_l", [P, CHUNK], F32R)
        h32 = sb("h32", [P, 2, CHUNK])
        h_h, h_l = sb("h_h", [P, HB, CHUNK], F32R), sb("h_l", [P, HB, CHUNK], F32R)
        rt = sb("rt", [P, CHUNK])
        st6 = sb("st6", [P, QT, 6])
        mv = sb("mv", [P, QT, 2])
        var_e = sb("var_e", [P, QT])
        nmean = sb("nmean", [P, QT])
        rstd = sb("rstd", [P, NT])
        nmr = sb("nmr", [P, QT])
        rows = sb("rows", [P, 2, NT, ROW])
        bst = rows[0:E, 0].rearrange("p t r -> p (t r)")[:, 0:H + D]
        lg = sb("lg", [P, NT, E])
        m12 = sb("m12", [P, 2, NTP])
        s12 = sb("s12", [P, 2, NTP])
        n = NTP * E
        oh = late[:, 0:2 * n].rearrange("p (k t e) -> p k t e", k=2, e=E)
        lg2, dst = (late[:, i * n:(i + 1) * n].rearrange("p (t e) -> p t e", e=E) for i in (2, 3))
        hits, incl = (late[:, i * n:(i + 1) * n] for i in (4, 5))
        eq, sc = (early[:, i * n:(i + 1) * n].rearrange("p (t e) -> p t e", e=E) for i in range(2))
        dk = sb("dk", [P, 2, NTP])
        slot_i = sb("slot_i", [P, 2, NT], U32)
        xin, xex = (early[:, 2 * n + i * NTP * (E + 1):2 * n + (i + 1) * NTP * (E + 1)] for i in range(2))
        den = sb("den", [P, NTP])
        rden = sb("rden", [P, NTP])
        cnt = sb("cnt", [P, 8, E])
        at = 2 * n + 2 * NTP * (E + 1)
        cmp = early[:, at:at + MMAX * E].rearrange("p (m e) -> p m e", e=E)
        ej = sb("ej", [P, MMAX])
        expert = sb("expert", [P, MT + 2])
        pair = sb("pair", [P, MT])
        experts = sb("experts", [P, MT], I32)
        ht_h = [h_h[:, b, 0:SLOTS] for b in range(HB)]
        ht_l = [h_l[:, b, 0:SLOTS] for b in range(HB)]
        xb = late[:, 4 * CHUNK - 2 * SQ * ROW:].rearrange("p (k q r) -> p k q r", k=2, q=SQ)
        xbt_h = [xt_h[:, k, 0:SLOTS] for k in range(2)]
        xbt_l = [xt_l[:, k, 0:SLOTS] for k in range(2)]
        yt = rt
        wslot = sb("wslot", [P, MT * SQ])
        dest = sb("dest", [P, MT * SQ], U32)
        sent = rows[:, 1].rearrange("p t r -> p (t r)")

        def y01(c):
            place, at = (sent, c) if c < PARTS[0] else (work, c - PARTS[0])
            return place[:, 2 * at * CHUNK:2 * (at + 1) * CHUNK].rearrange("p (a n) -> p a n", a=2)

        r3 = late[:, 0:FB * CHUNK].rearrange("p (k q d) -> p k q d", k=FB, q=QT)
        res = fw[:, :, :].rearrange("p e h -> p (e h)")[:, 0:NCH * CHUNK].bitcast(F32).rearrange("p (c q d) -> p c q d", c=NCH, q=QT)
        FQ = FB * QT
        f_st6 = early[:, 0:6 * FQ].rearrange("p (k q n) -> p k q n", k=FB, q=QT)
        f_mv = early[:, 6 * FQ:8 * FQ].rearrange("p (k q n) -> p k q n", k=FB, q=QT)
        f_var, f_nmean, f_rstd, f_nmr = (early[:, n * FQ:(n + 1) * FQ].rearrange("p (k q) -> p k q", k=FB) for n in range(8, 12))
        SUM_PS = [bank[i] for i in (1, 2, 0, 3, 4, 7)]

        names = """zero_ready const_ready par_loaded b_loaded aw_loaded
            exps_ready negnu_ready decay_ready om_ready gam_ready dve_link pool_link ones_ready sig_exp cs_ready
            tables_ready cc_ready setup_t setup_sb w_ready wgm_ready wgc_ready fw_hi fw_lo
            xT_ready xt_sb x_lo bu_ready p_ready u_ready q_ready y_ready y_hi y_lo
            pre_a h_act hh_ready hl_ready z_ready r_ready st_ready mv_ready ve_ready rstd_ready nmr_ready
            rt_ready row0_ready row1_ready lg_ready lg_sb
            hits_ready rank_ready rank_sb xin_ready xex_ready routed route_ready
            dispatched0 dispatched1 prefilled bias_loaded biasT_ready fbias_ready
            xTb_ready meta_ready w1use_ready w2use_ready xb_hi xb_lo preb_ready gelu_b hbh_ready hbh1_ready hbl_ready
            zb_ready yt_ready yT_ready yo_ready
            f_sum f_r f_st f_mv f_ve f_rstd f_nmr f_res f_res_last""".split()
        sm = {n: sem(n) for n in names}
        xr_loaded = [sem(f"xr_loaded{i}") for i in range(2)]
        fst_loaded = [sem(f"fst_loaded{i}") for i in range(2)]
        xb_loaded = [sem(f"xb_loaded{i}") for i in range(2)]
        kept = MT - YO
        GROUP = kept // 3
        assert kept % 3 == 0 and slots[0] <= kept
        returned = [sem(f"returned{i}") for i in range(4)]
        y0_loaded = [sem(f"y0_loaded{i}") for i in range(NCH)]
        y1_loaded = [sem(f"y1_loaded{i}") for i in range(NCH)]
        stored = sem("stored")

        NFW = 2 * E

        def pieces(c):
            return range(*PIECES[c:c + 2]) if c + 1 < len(PIECES) else range(0)

        def fw_src(n):
            return FW1[n] if n < E else FW2[n - E].rearrange("(c p) d -> p c d", p=P)

        def fw_stage(n):
            return fst[:, n % 2, :]

        def fw_stage_in(n):
            return fst[:, n % 2, :] if n < E else fst[:, n % 2, :].rearrange("p (c d) -> p c d", c=HB)

        def fw_dst(n, part):
            place = 2 * (n // E) + part
            return fw[:, n % E, place * H:(place + 1) * H]

        def wait_loaded(eng, g, k):
            eng.wait_ge(xb_loaded[k], 8 * (g - k) + 16)

        block = ctx.enter_context(nc.Block())

        @block.sync
        def _(sp):
            def over_states(src):
                return bass.AP(tensor=src.tensor, offset=0, ap=[[0, 4], [1, NS], [1, 1]])

            sp.dma_start(logs[:, 0:1], over_states(theta_log)).then_inc(sm["par_loaded"], 16)
            sp.dma_start(logs[:, 1:2], over_states(nu_log)).then_inc(sm["par_loaded"], 16)
            sp.dma_start(logs[:, 2:3], bass.AP(tensor=res_logit.tensor, offset=0, ap=[[0, P], [1, 1]])).then_inc(sm["par_loaded"], 16)
            for k in range(4):
                sp.dma_start(ball[k * NS:(k + 1) * NS, :], B_re if k in (0, 3) else B_im).then_inc(sm["b_loaded"], 16)
            sp.dma_start(xr[:, 0], x_t[0]).then_inc(xr_loaded[0], 16)
            sp.dma_start(cre[:], C_re).then_inc(sm["b_loaded"], 16)
            sp.dma_start(cim[:], C_im).then_inc(sm["b_loaded"], 16)
            sp.dma_start(dm[:], D_mat).then_inc(sm["b_loaded"], 16)
            sp.dma_start(xr[:, 1], x_t[1]).then_inc(xr_loaded[1], 16)
            sp.dma_start(aw_st[:, 0, :], W1).then_inc(sm["aw_loaded"], 16)
            sp.dma_start(aw_st[:, 1, :].rearrange("p (c d) -> p c d", c=HB),
                         W2.rearrange("(c p) d -> p c d", p=P)).then_inc(sm["aw_loaded"], 16)
            sp.dma_start(wg[:], Wg).then_inc(sm["bias_loaded"], 16)
            sp.dma_start(bst[:, 0:H], fb1).then_inc(sm["bias_loaded"], 16)
            sp.dma_start(bst[:, H:H + D], fb2).then_inc(sm["bias_loaded"], 16)

            def weights(n):
                wait(sp, sm["fw_lo"], n - 1)
                sp.dma_start(fw_stage_in(n), fw_src(n)).then_inc(fst_loaded[n % 2], 16)

            for n in range(2):
                weights(n)
            blocks = MT * SQ // 4
            sp.wait_ge(sm["zero_ready"], 1)
            padding = slots_d.rearrange("(p a b) r -> p a (b r)", p=P, b=4)

            def x_load(c):
                sp.wait_ge(sm["xT_ready"], c - 1)
                sp.dma_start(xr[:, c % 2], x_t[c]).then_inc(xr_loaded[c % 2], 16)

            x_load(2)
            x_load(3)
            for c in range(NCH):
                if c < PADS:
                    a, b = blocks * c // PADS, blocks * (c + 1) // PADS
                    sp.dma_start(padding[:, a:b], zeros[:, :].rearrange("p (a n) -> p a n", a=1).to_broadcast([P, b - a, 4 * ROW])
                                 ).then_inc(sm["prefilled"], 16)
                for n in pieces(c):
                    if n + 2 < NFW:
                        weights(n + 2)
                if c + 4 < NCH:
                    x_load(c + 4)

            sp.wait_ge(sm["fw_lo"], NFW)

            def load(g, k):
                wait(sp, sm["xTb_ready"], g - 1)
                wait(sp, sm["meta_ready"], g - 1)
                sp.dma_start(xb[:, k], slots_d[bass.ds(g * SLOTS, SLOTS), :].rearrange("(q p) r -> p q r", p=P)).then_inc(xb_loaded[k], 16)

            def loads(a, b):
                if (b - a) % 2:
                    load(a, a % 2)
                    a += 1
                with sp.Fori(0, (b - a) // 2) as i:
                    for k in range(2):
                        load(2 * i + (a + k), (a + k) % 2)

            sp.wait_ge(sm["dispatched0"], 16 * 2 * tiles[0])
            load(0, 0)
            load(1, 1)
            loads(2, slot0[1])
            sp.wait_ge(sm["dispatched1"], 16 * 2 * tiles[1])
            loads(slot0[1], MT)

            def results(c):
                src = results_d[0:2 * T, :].rearrange("(a c q p) d -> c a p q d", a=2, q=QT, p=P)[c]
                for a in range(2):
                    sp.dma_start(y01(c)[:, a].rearrange("p (q d) -> p q d", q=QT), src[a]).then_inc((y0_loaded, y1_loaded)[a][c], 16)

            for i in range(3):
                sp.wait_ge(returned[i], 16 * SQ * GROUP)
            for c in range(PARTS[0]):
                results(c)
            sp.wait_ge(returned[3], 16 * SQ * YO)
            for c in range(PARTS[0], NCH):
                results(c)
            for c in range(NCH):
                sp.wait_ge(sm["f_res"], c + 1)
                if c == NCH - 1:
                    sp.wait_ge(sm["f_res_last"], 1)
                sp.dma_start(out_t[c], res[:, c]).then_inc(stored, 16)
            sp.wait_ge(stored, 16 * NCH)
            sp.wait_ge(sm["prefilled"], 16 * PADS)

        @block.gpsimd
        def _(pool):
            pool.memset(ident[:], 0.0).then_inc(sm["pool_link"], 1)
            pool.memset(base_e[:], 2.718281828459045)
            pool.memset(minus[:], -1.0)
            pool.memset(halves[:], 0.5)
            pool.memset(mhalves[:], -0.5).then_inc(sm["pool_link"], 1)
            pool.iota(steps[:], [[1, S]], base=0, channel_multiplier=0, allow_small_or_imprecise_dtypes=True).then_inc(sm["const_ready"], 1)
            pool.wait_ge(sm["par_loaded"], 16 * 3)
            pool.wait_ge(sm["pool_link"], 2)
            pool.tensor_tensor(exps[:, 0:2], base_e[:, 0:2], logs[:, 0:2], ALU.pow).then_inc(sm["exps_ready"], 1)
            pool.wait_ge(sm["exps_ready"], 1)
            pool.tensor_tensor(negnu[:], exps[:, 1:2], minus[:, 0:1], ALU.mult).then_inc(sm["negnu_ready"], 1)
            pool.wait_ge(sm["negnu_ready"], 1)
            pool.tensor_tensor(decay[:], base_e[:, 0:1], negnu[:], ALU.pow).then_inc(sm["decay_ready"], 1)
            pool.affine_select(out=ident[:], in_=ident[:], compare_op=ALU.not_equal, fill=1.0, base=0,
                               pattern=[[-1, P]], channel_multiplier=1).then_inc(sm["const_ready"], 1)
            pool.wait_ge(sm["om_ready"], 1)
            pool.tensor_tensor(gam[:], om[:], halves[:, 0:1], ALU.pow).then_inc(sm["gam_ready"], 1)
            pool.tensor_tensor(exps[:, 2:3], logs[:, 2:3], minus[:, 0:1], ALU.mult).then_inc(sm["pool_link"], 1)
            pool.wait_ge(sm["pool_link"], 3)
            pool.tensor_tensor(sgl[:, 1:2], base_e[:, 0:1], exps[:, 2:3], ALU.pow).then_inc(sm["sig_exp"], 1)
            pool.memset(zeros[:], 0.0).then_inc(sm["zero_ready"], 1)
            pool.memset(ones[:], 1.0).then_inc(sm["pool_link"], 1)
            pool.memset(expert[:], 0.0)
            pool.memset(restart[:], 1.0).then_inc(sm["pool_link"], 1)
            pool.memset(epss[:, 0:4], EPS / 4)
            pool.memset(epss[:, 4:8], EPS).then_inc(sm["ones_ready"], 1)
            pool.wait_ge(sm["pool_link"], 5)
            pool.affine_select(out=before[:], in_=ones[:], compare_op=ALU.is_gt, fill=0.0, base=0,
                               pattern=[[1, P]], channel_multiplier=-1).then_inc(sm["const_ready"], 1)
            pool.iota(rev[:], [[-1, E]], base=E, channel_multiplier=0, allow_small_or_imprecise_dtypes=True)
            pool.iota(tok[:], [[P, NT]], base=0, channel_multiplier=1, allow_small_or_imprecise_dtypes=True)
            pool.iota(dump[:], [[P, MT * SQ]], base=2 * T, channel_multiplier=1, allow_small_or_imprecise_dtypes=True)
            pool.iota(jio[:], [[1, MMAX]], base=0, channel_multiplier=0, allow_small_or_imprecise_dtypes=True)
            pool.memset(restart[:, :].rearrange("p (e t) -> p e t", e=E)[:, :, 0:1], 0.0).then_inc(sm["const_ready"], 1)

            def weights(n):
                pool.wait_ge(fst_loaded[n % 2], 16 * (n // 2 + 1))
                pool.tensor_copy(fw_dst(n, 0), fw_stage(n)).then_inc(sm["fw_hi"], 1)
                pool.wait_ge(sm["fw_hi"], n + 1)
                pool.tensor_tensor(fw_dst(n, 1), fw_stage(n), fw_dst(n, 0).bitcast(F32), ALU.subtract).then_inc(sm["fw_lo"], 1)

            def norm(c):
                pool.wait_ge(sm["mv_ready"], QT * (c + 1))
                wait(pool, sm["row0_ready"], c)
                pool.tensor_tensor(var_e[:], mv[:, :, 1], epss[:, 0:4], ALU.add).then_inc(sm["ve_ready"], 1)
                pool.tensor_tensor(nmean[:], mv[:, :, 0], minus[:], ALU.mult)
                pool.wait_ge(sm["ve_ready"], c + 1)
                pool.tensor_tensor(rstd[:, QT * c:QT * (c + 1)], var_e[:], mhalves[:], ALU.pow).then_inc(sm["rstd_ready"], 1)
                pool.wait_ge(sm["rstd_ready"], c + 1)
                pool.tensor_tensor(nmr[:], nmean[:], rstd[:, QT * c:QT * (c + 1)], ALU.mult).then_inc(sm["nmr_ready"], 1)

            def dispatch(p, i):
                for k in range(2):
                    pool.indirect_dma_start(out=slots_d, out_offset=bass.IndirectOffsetOnAxis(ap=slot_i[:, k, i:i + 1], axis=0),
                                            in_=rows[:, k, i, :], in_offset=None).then_inc(sm[f"dispatched{p}"], 16)

            def send_back(g):
                pool.wait_ge(sm["yo_ready"], g + 1)
                for q in range(SQ):
                    pool.indirect_dma_start(out=results_d, out_offset=bass.IndirectOffsetOnAxis(ap=dest[:, SQ * g + q:SQ * g + q + 1], axis=0),
                                            in_=yo[:, g % YO, q, :], in_offset=None).then_inc(returned[min(g // GROUP, 3)], 16)

            routed = PARTS[0] + 1
            first = 0
            for c in range(NCH + 2):
                if c > routed:
                    if c == routed + 1:
                        pool.wait_ge(sm["prefilled"], 16 * PADS)
                        pool.wait_ge(sm["routed"], 1)
                        pool.wait_ge(sm["row1_ready"], PARTS[0])
                    last = min(4 * (c - routed) - 2, tiles[0])
                    for i in range(first, last):
                        dispatch(0, i)
                    first = last
                if c >= 2:
                    norm(c - 2)
                for n in pieces(c):
                    weights(n)
            pool.wait_ge(sm["routed"], 2)
            pool.wait_ge(sm["row1_ready"], NCH)
            for i in range(tile0[1], NT):
                dispatch(1, i)
            for g in range(MT):
                send_back(g)

            def final_norm(c, k):
                pool.wait_ge(sm["f_mv"], QT * c + QT)
                wait(pool, sm["f_res"], c + 1 - FB)
                pool.tensor_tensor(f_var[:, k], f_mv[:, k, :, 1], epss[:, 4:8], ALU.add).then_inc(sm["f_ve"], 1)
                pool.tensor_tensor(f_nmean[:, k], f_mv[:, k, :, 0], minus[:], ALU.mult)
                pool.wait_ge(sm["f_ve"], c + 1)
                pool.tensor_tensor(f_rstd[:, k], f_var[:, k], mhalves[:], ALU.pow).then_inc(sm["f_rstd"], 1)
                pool.wait_ge(sm["f_rstd"], c + 1)
                pool.tensor_tensor(f_nmr[:, k], f_nmean[:, k], f_rstd[:, k], ALU.mult).then_inc(sm["f_nmr"], 1)

            for c in range(NCH):
                final_norm(c, c % FB)

        @block.scalar
        def _(act):
            def x_copy(c):
                act.wait_ge(sm["xT_ready"], c + 1)
                wait(act, sm["r_ready"], c - 2)
                act.copy(xt32[:, c % 3, :], XT_PS[:])
                wait(act, sm["y_ready"], c - 1)
                act.copy(xt_h[:, c % 2, :], XT_PS[:]).then_inc(sm["xt_sb"], 1)

            def rows_of(c):
                act.wait_ge(sm["nmr_ready"], c + 1)
                for q in range(QT):
                    i = QT * c + q
                    last = act.activation(rows[:, 0, i, 0:D], R_PS[:, q * D:(q + 1) * D], ACT.Identity, bias=nmr[:, q:q + 1], scale=rstd[:, i:i + 1])
                last.then_inc(sm["row0_ready"], 1)
                act.wait_ge(sm["row0_ready"], c + 1)
                act.copy(rows[:, 1, QT * c:QT * (c + 1), 0:D], rows[:, 0, QT * c:QT * (c + 1), 0:D]).then_inc(sm["row1_ready"], 1)

            def y_high(c):
                act.wait_ge(sm["y_ready"], c + 1)
                wait(act, sm["pre_a"], HB * c)
                act.copy(y_h[:], Y_PS[:]).then_inc(sm["y_hi"], 1)

            def x_high(g, k):
                act.wait_ge(sm["xTb_ready"], g + 1)
                wait(act, sm["preb_ready"], HB * (g - 1))
                act.copy(xbt_h[k], XTB_PS[:, 0:SLOTS]).then_inc(sm["xb_hi"], 1)

            def chunk(c):
                for b in range(HB):
                    n = HB * c + b
                    act.wait_ge(sm["pre_a"], n + 1)
                    wait(act, sm["hl_ready"], n - 1)
                    act.activation(h32[:, b % 2, :], H_PS[b % 2][:], ACT.Gelu_apprx_tanh).then_inc(sm["h_act"], 1)
                    act.wait_ge(sm["h_act"], n + 1)
                    wait(act, sm["z_ready"], n + 1 - HB)
                    act.copy(h_h[:, b, :], h32[:, b % 2, :]).then_inc(sm["hh_ready"], 1)
                    if b == 1 and c + 2 < NCH:
                        x_copy(c + 2)
                if c == PARTS[0] + 1:
                    softmax_exp(0)
                    act.preload_act_table_set("gelu_apprx_tanh_and_others")
                if c + 1 < NCH:
                    y_high(c + 1)
                if c >= 2:
                    rows_of(c - 2)

            def softmax_exp(p):
                act.wait_ge(sm["xin_ready"], p + 1)
                n = tiles[p] * (E + 1)
                act.activation(xex[:, 0:n], xin[:, 0:n], ACT.Exp).then_inc(sm["xex_ready"], 1)

            act.wait_ge(sm["b_loaded"], 16 * 7)
            for a, b, src, sign in ((0, 0, cre, 1.0), (0, 1, cim, -1.0), (1, 0, cim, -1.0), (1, 1, cre, -1.0)):
                places = cc[:, a, :].rearrange("p (r b n) -> p r b n", r=2, b=2)[:, :, b, :]
                act.activation(places, src[:, :].rearrange("p (a n) -> p a n", a=1).to_broadcast([P, 2, NS]),
                               ACT.Copy, scale=sign).then_inc(sm["cc_ready"], 1)
            x_copy(0)
            act.wait_ge(sm["tables_ready"], 1)
            act.activation(cs[:, :, :].rearrange("p a s -> p (a s)"), ph[:, :, :].rearrange("p a s -> p (a s)"),
                           ACT.Sin, scale=TWO_PI).then_inc(sm["cs_ready"], 1)
            x_copy(1)
            act.preload_act_table_set("gelu_apprx_tanh_and_others")
            y_high(0)
            for c in range(NCH):
                chunk(c)
            act.preload_act_table_set("gelu_and_others")

            def evacuate(g, k):
                act.wait_ge(sm["zb_ready"], HB * (g + 1))
                wait(act, sm["yT_ready"], g)
                act.activation(yt[:, 0:SLOTS], ZB_PS[k][:, 0:SLOTS], ACT.Identity,
                               bias=buse[:, k, HB:HB + 1]).then_inc(sm["yt_ready"], 1)

            def step(g, k, now, prev, nxt, far, nth):
                if prev and not now:
                    evacuate(g - 1, 1 - k)
                if now:
                    act.wait_ge(sm["w2use_ready"], g + 1)
                    for b in range(HB):
                        act.wait_ge(sm["preb_ready"], HB * g + (b + 1))
                        wait(act, sm["hbl_ready"], HB * g + (b - 1))
                        act.activation(h32[:, b % 2, 0:SLOTS], H_PS[b % 2][:, 0:SLOTS], ACT.Gelu,
                                       bias=buse[:, k, b:b + 1]).then_inc(sm["gelu_b"], 1)
                        if b % 2 == 0:
                            act.wait_ge(sm["gelu_b"], HB * g + (b + 1))
                            wait(act, sm["zb_ready"], HB * g + (b + 1 - HB))
                            act.copy(ht_h[b], h32[:, b % 2, 0:SLOTS]).then_inc(sm["hbh_ready"], 1)
                        if b == 1 and prev:
                            evacuate(g - 1, 1 - k)
                        if b == 1 and nxt:
                            x_high(g + 1, 1 - k)
                if prev:
                    act.wait_ge(sm["yT_ready"], g)
                    act.wait_ge(sm["meta_ready"], g)
                    for q in range(SQ):
                        i = (g - 1) * SQ + q
                        w = wslot[:, i:i + 1] if isinstance(i, int) else wslot[:, bass.ds(i, 1)]
                        last = act.activation(row_of_yo(g - 1, q), YB_PS[1 - k][:, q * D:(q + 1) * D], ACT.Copy, scale=w)
                    last.then_inc(sm["yo_ready"], 1)

            def row_of_yo(g, q):
                if isinstance(g, int):
                    return yo[:, g % YO, q, :]
                return yo[:, bass.ds(g % YO, 1), q, :].rearrange("p a d -> p (a d)")

            def second_exp():
                softmax_exp(1)
                act.preload_act_table_set("gelu_and_others")

            x_high(0, 0)
            rows_of(NCH - 2)

            def sent_back(i):
                return lambda: act.wait_ge(returned[i], 16 * SQ * GROUP)

            walk(act, MT, step, {ROUTE1: lambda: act.wait_ge(sm["rt_ready"], NCH),
                                 ROUTE1 + 1: lambda: rows_of(NCH - 1), ROUTE1 + 3: second_exp,
                                 **{YO + 1 + GROUP * i: sent_back(i) for i in range(3)}})

            def final_apply(c, k):
                act.wait_ge(sm["f_nmr"], c + 1)
                for q in range(QT if c < NCH - 1 else QT // 2):
                    last = act.activation(res[:, c, q, :], r3[:, k, q, :], ACT.Identity, bias=f_nmr[:, k, q:q + 1], scale=f_rstd[:, k, q:q + 1])
                last.then_inc(sm["f_res"], 1)

            for c in range(NCH):
                final_apply(c, c % FB)

        @block.vector
        def _(dve):
            chain = [0]

            def link(ins):
                chain[0] += 1
                ins.then_inc(sm["dve_link"], 1)
                dve.wait_ge(sm["dve_link"], chain[0])

            dve.wait_ge(sm["exps_ready"], 1)
            link(dve.tensor_scalar(turn[:, 0:1], exps[:, 0:1], 0.15915494309189535, None, ALU.mult))
            link(dve.tensor_scalar(turn[:, 1:2], turn[:, 0:1], ROUND, -ROUND, ALU.add, ALU.add))
            link(dve.tensor_tensor(turn[:, 0:1], turn[:, 0:1], turn[:, 1:2], ALU.subtract))
            link(dve.tensor_scalar(turn[:, 2:3], turn[:, 0:1], ROUND15, -ROUND15, ALU.add, ALU.add))
            link(dve.tensor_tensor(turn[:, 3:4], turn[:, 0:1], turn[:, 2:3], ALU.subtract))
            dve.wait_ge(sm["decay_ready"], 1)
            link(dve.tensor_tensor(om[:], decay[:], decay[:], ALU.mult))
            dve.tensor_scalar(om[:], om[:], -1.0, 1.0, ALU.mult, ALU.add).then_inc(sm["om_ready"], 1)
            dve.wait_ge(sm["const_ready"], 1)
            link(dve.tensor_scalar(ph[:, 0, :], steps[:], turn[:, 2:3], None, ALU.mult))
            link(dve.tensor_scalar(ph2[:, 0, :], ph[:, 0, :], ROUND, -ROUND, ALU.add, ALU.add))
            link(dve.tensor_tensor(ph[:, 1, :], ph[:, 0, :], ph2[:, 0, :], ALU.subtract))
            link(dve.scalar_tensor_tensor(out=ph2[:, 1, :], in0=steps[:], scalar=turn[:, 3:4], in1=ph[:, 1, :], op0=ALU.mult, op1=ALU.add))
            link(dve.tensor_scalar(ph2[:, 0, :], ph2[:, 1, :], 0.25, None, ALU.add))
            link(dve.tensor_scalar(cs[:, :, :], ph2[:, :, :], ROUND, -ROUND, ALU.add, ALU.add))
            dve.tensor_tensor(ph[:, :, :], ph2[:, :, :], cs[:, :, :], ALU.subtract).then_inc(sm["tables_ready"], 1)
            link(dve.tensor_scalar(rdec[:, :, :], ph2[:, :, :], 0.0, decay[:, 0:1], ALU.mult, ALU.add))
            link(dve.memset(rdec[:, :, 0:1], 0.0))
            dve.wait_ge(sm["setup_t"], 1)
            dve.tensor_copy(bt_h[:], Z_PS[:, 0:P])
            dve.tensor_copy(dt_h[:], Z_PS[:, P:2 * P])
            link(dve.tensor_copy(wcs[:, :, :].rearrange("p a n -> p (a n)"), Z_PS[:, 2 * P:4 * P]))
            dve.tensor_tensor(bt_l[:], Z_PS[:, 0:P], bt_h[:].bitcast(F32), ALU.subtract)
            dve.tensor_tensor(dt_l[:], Z_PS[:, P:2 * P], dt_h[:].bitcast(F32), ALU.subtract).then_inc(sm["setup_sb"], 1)
            def x_split(c):
                dve.wait_ge(sm["xt_sb"], c + 1)
                dve.tensor_tensor(xt_l[:, c % 2, :], xt32[:, c % 3, :], xt_h[:, c % 2, :].bitcast(F32), ALU.subtract).then_inc(sm["x_lo"], 1)

            dve.wait_ge(sm["cs_ready"], 1)
            x_split(0)
            dve.wait_ge(sm["gam_ready"], 1)
            link(dve.tensor_scalar(gam[96:P, :], gam[96:P, :], -1.0, None, ALU.mult))
            dve.tensor_scalar(tin[0:64, :], cs[0:64, 0, :], gam[0:64, 0:1], None, ALU.mult)
            link(dve.tensor_scalar(tin[64:P, :], cs[64:P, 1, :], gam[64:P, 0:1], None, ALU.mult))

            def both(t):
                return t.rearrange("p (a s) -> p a s", a=1).to_broadcast([P, 2, S])

            def two(t):
                return t.rearrange("p (a s) -> p a s", a=2)

            def turn_in(c):
                dve.wait_ge(sm["bu_ready"], c + 1)
                dve.tensor_tensor(two(pt), two(BU_PS[:, :]), both(tin[:, :]), ALU.mult).then_inc(sm["p_ready"], 1)
                dve.wait_ge(sm["p_ready"], c + 1)
                dve.tensor_tensor_scan(ut, rdec[:, :, :].rearrange("p a s -> p (a s)"), pt, 0.0, ALU.mult, ALU.add).then_inc(sm["u_ready"], 1)

            def turn_back(c, n):
                dve.wait_ge(sm["u_ready"], c + 1)
                wait(dve, sm["y_ready"], c)
                dve.tensor_tensor(two((qc, qs)[n]), two(ut), both(cs[:, n, :]), ALU.mult).then_inc(sm["q_ready"], 1)

            def hidden_low(c, b):
                dve.wait_ge(sm["hh_ready"], HB * c + b + 1)
                dve.tensor_tensor(h_l[:, b, :], h32[:, b % 2, :], h_h[:, b, :].bitcast(F32), ALU.subtract).then_inc(sm["hl_ready"], 1)

            def stats(c):
                dve.wait_ge(sm["rt_ready"], c + 1)
                for q in range(QT):
                    dve.bn_stats(st6[:, q, :], R_PS[:, q * D:(q + 1) * D]).then_inc(sm["st_ready"], 1)

            def aggregate(c):
                dve.wait_ge(sm["st_ready"], QT * (c + 1))
                wait(dve, sm["nmr_ready"], c)
                for q in range(QT):
                    dve.bn_aggr(mv[:, q, :], st6[:, q, :]).then_inc(sm["mv_ready"], 1)

            def logits(c):
                dve.wait_ge(sm["lg_ready"], c + 1)
                dve.tensor_copy(lg[:, QT * c:QT * (c + 1), :].rearrange("p q e -> p (q e)"), LG_PS[:, 0:QT * E]).then_inc(sm["lg_sb"], 1)

            def y_low(c):
                dve.wait_ge(sm["y_hi"], c + 1)
                dve.tensor_tensor(y_l[:], Y_PS[:], y_h[:].bitcast(F32), ALU.subtract).then_inc(sm["y_lo"], 1)

            def chunk(c):
                if c + 1 < NCH:
                    turn_back(c + 1, 0)
                    turn_back(c + 1, 1)
                if c == PARTS[0] + 1:
                    route_choice(0, 1)
                    route_hits(0)
                    route_exponents(0)
                    logits(c - 1)
                hidden_low(c, 0)
                hidden_low(c, 1)
                if c == PARTS[0] + 1:
                    route_ranks(0)
                    route_slots(0)
                if c + 2 < NCH:
                    x_split(c + 2)
                hidden_low(c, 2)
                if c >= 1 and c != PARTS[0] + 1:
                    logits(c - 1)
                hidden_low(c, 3)
                if c == PARTS[0] + 1:
                    route_weights(0)
                if c + 1 < NCH:
                    y_low(c + 1)
                if c == PARTS[0]:
                    route_choice(0, 0)
                if c + 2 < NCH:
                    turn_in(c + 2)
                if c == PARTS[0] + 1:
                    route_experts(0)
                dve.wait_ge(sm["z_ready"], HB * (c + 1))
                wait(dve, sm["rt_ready"], c)
                dve.scalar_tensor_tensor(out=rt[:], in0=Z_PS[:], scalar=sgl[:, 2:3], in1=xt32[:, c % 3, :],
                                         op0=ALU.mult, op1=ALU.add).then_inc(sm["r_ready"], 1)
                if c >= 1:
                    stats(c - 1)
                    aggregate(c - 1)


            def over_e(t, n):
                return t.rearrange("p (n a) -> p n a", a=1).to_broadcast([P, n, E])

            def route_choice(p, k):
                n, t0 = tiles[p], tile0[p]
                lgp = lg[:, t0:t0 + n, :]
                if k == 0:
                    dve.wait_ge(sm["lg_sb"], starts[p] + PARTS[p])
                    src = lgp
                else:
                    src = lg2[:, 0:n, :]
                    link(dve.scalar_tensor_tensor(out=src, in0=oh[:, 0, 0:n, :], scalar=-BIG, in1=lgp, op0=ALU.mult, op1=ALU.add))
                link(dve.tensor_reduce(m12[:, k, 0:n], src, AX_X, ALU.max))
                link(dve.tensor_tensor(eq[:, 0:n, :], src, over_e(m12[:, k, 0:n], n), ALU.is_equal))
                link(dve.tensor_tensor(sc[:, 0:n, :], eq[:, 0:n, :], rev[:, :].rearrange("p (a e) -> p a e", a=1).to_broadcast([P, n, E]), ALU.mult))
                link(dve.tensor_reduce(s12[:, k, 0:n], sc[:, 0:n, :], AX_X, ALU.max))
                link(dve.tensor_tensor(oh[:, k, 0:n, :], sc[:, 0:n, :], over_e(s12[:, k, 0:n], n), ALU.is_equal))

            def route_hits(p):
                n, t0 = tiles[p], tile0[p]
                hv, iv = hits[:, 0:E * n], incl[:, 0:E * n]
                link(dve.tensor_tensor(hv.rearrange("p (e t) -> p t e", e=E), oh[:, 0, 0:n, :], oh[:, 1, 0:n, :], ALU.add))
                rs = restart[:]
                if n != NTP:
                    rs = cmp[:, :, :].rearrange("p a b -> p (a b)")[:, 0:E * n]
                    link(dve.tensor_copy(rs.rearrange("p (e t) -> p e t", e=E), restart[:, :].rearrange("p (e t) -> p e t", e=E)[:, :, 0:n]))
                link(dve.tensor_tensor_scan(iv, rs, hv, 0.0, ALU.mult, ALU.add))
                dve.tensor_copy(cnt[:, 0, :], iv.rearrange("p (e t) -> p e t", e=E)[:, :, n - 1]).then_inc(sm["hits_ready"], 1)

            def route_exponents(p):
                n, t0 = tiles[p], tile0[p]
                xl = xin[:, 0:n * E].rearrange("p (n e) -> p n e", e=E)
                x2 = xin[:, n * E:n * (E + 1)]
                dve.tensor_tensor(xl, lg[:, t0:t0 + n, :], over_e(m12[:, 0, 0:n], n), ALU.subtract)
                link(dve.tensor_tensor(x2, m12[:, 1, 0:n], m12[:, 0, 0:n], ALU.subtract))
                dve.wait_ge(sm["rstd_ready"], starts[p] + PARTS[p])
                dve.tensor_tensor(xl, xl, over_e(rstd[:, t0:t0 + n], n), ALU.mult)
                dve.tensor_tensor(x2, x2, rstd[:, t0:t0 + n], ALU.mult).then_inc(sm["xin_ready"], 1)

            def route_ranks(p):
                dve.wait_ge(sm["rank_ready"], p + 1)
                dve.tensor_copy(cnt[:, 6:8, :].rearrange("p a e -> p (a e)"), LG_PS[:, 0:2 * E]).then_inc(sm["rank_sb"], 1)
                dve.wait_ge(sm["rank_sb"], p + 1)
                link(dve.tensor_scalar(cnt[:, 1, :], cnt[:, 7, :], 1.0 / SLOTS, (SLOTS - 1) / 2 / SLOTS, ALU.mult, ALU.add))
                link(dve.tensor_scalar(cnt[:, 2, :], cnt[:, 1, :], ROUND, -ROUND, ALU.add, ALU.add))
                link(dve.tensor_tensor_scan(cnt[:, 3, :], ones[:, 0:E], cnt[:, 2, :], 0.0, ALU.mult, ALU.add))
                link(dve.tensor_tensor(cnt[:, 4, :], cnt[:, 3, :], cnt[:, 2, :], ALU.subtract))
                link(dve.scalar_tensor_tensor(out=cnt[:, 5, :], in0=cnt[:, 4, :], scalar=float(SLOTS), in1=cnt[:, 6, :], op0=ALU.mult, op1=ALU.add))

            def route_slots(p):
                n, t0 = tiles[p], tile0[p]
                off = slot0[p] * SLOTS - 1
                link(dve.tensor_tensor(dst[:, 0:n, :], incl[:, 0:E * n].rearrange("p (e t) -> p t e", e=E),
                                       cnt[:, 5:6, :].to_broadcast([P, n, E]), ALU.add))
                dve.tensor_tensor(eq[:, 0:n, :], oh[:, 0, 0:n, :], dst[:, 0:n, :], ALU.mult)
                link(dve.tensor_tensor(sc[:, 0:n, :], oh[:, 1, 0:n, :], dst[:, 0:n, :], ALU.mult))
                dve.tensor_reduce(dk[:, 0, 0:n], eq[:, 0:n, :], AX_X, ALU.add)
                link(dve.tensor_reduce(dk[:, 1, 0:n], sc[:, 0:n, :], AX_X, ALU.add))
                dve.tensor_scalar(slot_i[:, :, t0:t0 + n], dk[:, :, 0:n], float(off), None, ALU.add)
                for k in range(2):
                    ins = dve.scalar_tensor_tensor(out=s12[:, k, 0:n], in0=dk[:, k, 0:n], scalar=-1.0, in1=tok[:, t0:t0 + n], op0=ALU.mult, op1=ALU.add)
                link(ins)
                for k in range(2):
                    dve.tensor_scalar(rows[:, k, t0:t0 + n, D], s12[:, k, 0:n], float(k * T - 2 * T - off), None, ALU.add)

            def route_weights(p):
                n, t0 = tiles[p], tile0[p]
                dve.wait_ge(sm["xex_ready"], p + 1)
                link(dve.tensor_reduce(den[:, 0:n], xex[:, 0:n * E].rearrange("p (n e) -> p n e", e=E), AX_X, ALU.add))
                link(dve.reciprocal(rden[:, 0:n], den[:, 0:n]))
                dve.tensor_copy(rows[:, 0, t0:t0 + n, D + 1], rden[:, 0:n])
                dve.tensor_tensor(rows[:, 1, t0:t0 + n, D + 1], xex[:, n * E:n * (E + 1)], rden[:, 0:n], ALU.mult).then_inc(sm["routed"], 1)

            def route_experts(p):
                M, g0 = slots[p], slot0[p]
                link(dve.tensor_tensor(cmp[:, 0:M, :], jio[:, 0:M].rearrange("p (m a) -> p m a", a=1).to_broadcast([P, M, E]),
                                       cnt[:, 3:4, :].to_broadcast([P, M, E]), ALU.is_ge))
                link(dve.tensor_reduce(ej[:, 0:M], cmp[:, 0:M, :], AX_X, ALU.add))
                link(dve.tensor_scalar(expert[:, g0:g0 + M], ej[:, 0:M], float(E - 1), None, ALU.min))
                link(dve.scalar_tensor_tensor(out=pair[:], in0=expert[:, 1:MT + 1], scalar=float(E), in1=expert[:, 2:MT + 2], op0=ALU.mult, op1=ALU.add))
                dve.scalar_tensor_tensor(out=experts[:], in0=expert[:, 0:MT], scalar=float(E * E), in1=pair[:], op0=ALU.mult, op1=ALU.add).then_inc(sm["route_ready"], 1)

            turn_in(0)
            turn_back(0, 0)
            turn_back(0, 1)
            x_split(1)
            dve.wait_ge(sm["aw_loaded"], 32)
            dve.tensor_copy(w1_h, aw_st[:, 0, :])
            link(dve.tensor_copy(w2_h, aw_st[:, 1, :]))
            dve.tensor_tensor(w1_l, aw_st[:, 0, :], w1_h.bitcast(F32), ALU.subtract)
            dve.tensor_tensor(w2_l, aw_st[:, 1, :], w2_h.bitcast(F32), ALU.subtract).then_inc(sm["w_ready"], 1)
            dve.wait_ge(sm["sig_exp"], 1)
            link(dve.tensor_scalar(sgl[:, 2:3], sgl[:, 1:2], 1.0, None, ALU.add))
            link(dve.reciprocal(sgl[:, 3:4], sgl[:, 2:3]))
            link(dve.tensor_scalar(sgl[:, 2:3], sgl[:, 3:4], 0.5, None, ALU.mult))
            dve.wait_ge(sm["wgm_ready"], 1)
            dve.scalar_tensor_tensor(out=wgc[:], in0=LG_PS[:, 0:E], scalar=-1.0 / D, in1=wg[:], op0=ALU.mult, op1=ALU.add).then_inc(sm["wgc_ready"], 1)
            dve.wait_ge(sm["biasT_ready"], 1)
            dve.tensor_copy(fbias[:, :, :].rearrange("p e b -> p b e"), H_PS[0][:, 0:E * (HB + 1)].rearrange("p (b e) -> p b e", e=E)).then_inc(sm["fbias_ready"], 1)
            y_low(0)
            turn_in(1)
            dve.wait_ge(sm["const_ready"], 4)
            def experts_of(g):
                at = experts[0:1, g:g + 1] if isinstance(g, int) else experts[0:1, bass.ds(g, 1)]
                e = dve.value_load(at, min_val=0, max_val=E * E * E - 1)
                return [e // (E * E), (e // E) % E, e % E]

            def part_of_weights(k, e, a):
                return dve.tensor_copy(wuse[k][:, 2 * a:2 * a + 2, :].rearrange("p a h -> p (a h)"),
                                       fw[:, bass.ds(e, 1), 2 * a * H:2 * (a + 1) * H].rearrange("p a h -> p (a h)"))

            def weights1(g, k, e):
                wait(dve, sm["preb_ready"], HB * (g - 1))
                part_of_weights(k, e, 0).then_inc(sm["w1use_ready"], 1)

            def weights2(g, k, e):
                wait(dve, sm["zb_ready"], HB * (g - 1))
                part_of_weights(k, e, 1)
                wait(dve, sm["yt_ready"], g - 1)
                dve.tensor_copy(buse[:, k, :], fbias[:, bass.ds(e, 1), :].rearrange("p a b -> p (a b)")).then_inc(sm["w2use_ready"], 1)

            def meta(g, k):
                i = SQ * g
                cut = (lambda t: t[:, i:i + SQ]) if isinstance(g, int) else (lambda t: t[:, bass.ds(i, SQ)])
                wait_loaded(dve, g, k)
                dve.tensor_tensor(cut(dest), xb[:, k, :, D], cut(dump), ALU.add)
                dve.tensor_copy(cut(wslot), xb[:, k, :, D + 1]).then_inc(sm["meta_ready"], 1)

            def x_low(g, k):
                dve.wait_ge(sm["xb_hi"], g + 1)
                dve.tensor_tensor(xbt_l[k], XTB_PS[:, 0:SLOTS], xbt_h[k].bitcast(F32), ALU.subtract).then_inc(sm["xb_lo"], 1)

            held = []

            def step(g, k, now, prev, nxt, far, nth):
                if now:
                    for b in range(HB):
                        if b % 2:
                            dve.wait_ge(sm["gelu_b"], HB * g + (b + 1))
                            wait(dve, sm["zb_ready"], HB * g + (b + 1 - HB))
                            dve.tensor_copy(ht_h[b], h32[:, b % 2, 0:SLOTS]).then_inc(sm["hbh1_ready"], 1)
                            dve.wait_ge(sm["hbh1_ready"], 2 * g + (b // 2 + 1))
                        else:
                            dve.wait_ge(sm["hbh_ready"], 2 * g + (b // 2 + 1))
                        dve.tensor_tensor(ht_l[b], h32[:, b % 2, 0:SLOTS], ht_h[b].bitcast(F32), ALU.subtract).then_inc(sm["hbl_ready"], 1)
                        if b == 0 and nxt and nth != 1:
                            held[:] = experts_of(g + 1)
                        e = held[1:] if nth == 1 else held
                        if b == 1 and nxt:
                            x_low(g + 1, 1 - k)
                            weights2(g + 1, 1 - k, e[0])
                            meta(g + 1, 1 - k)
                        if b == 3 and far:
                            weights1(g + 2, k, e[1])

            for c in range(NCH):
                chunk(c)
                if c == NCH - 2:
                    dve.wait_ge(sm["fw_lo"], NFW)
                    dve.wait_ge(sm["route_ready"], 1)
                    e = experts_of(0)
                    weights1(0, 0, e[0])
                    weights2(0, 0, e[0])
            logits(NCH - 1)
            route_choice(1, 0)
            x_low(0, 0)
            weights1(1, 1, e[1])
            meta(0, 0)
            route_choice(1, 1)

            def last_stats():
                stats(NCH - 1)
                aggregate(NCH - 1)
                route_hits(1)

            def second_ranks():
                route_exponents(1)
                route_ranks(1)

            def second_weights():
                route_weights(1)
                route_experts(1)
                dve.wait_ge(sm["route_ready"], 2)

            walk(dve, MT, step, {ROUTE1: last_stats, ROUTE1 + 1: second_ranks,
                                 ROUTE1 + 2: lambda: route_slots(1), ROUTE1 + 3: second_weights})

            def final_sum(c, k):
                wait(dve, sm["f_res"], c + 1 - FB)
                dve.wait_ge(sm["f_sum"], c + 1)
                dve.wait_ge(y1_loaded[c], 16)
                dve.tensor_tensor(r3[:, k].rearrange("p q d -> p (q d)"), SUM_PS[c % len(SUM_PS)][:], y01(c)[:, 1], ALU.add).then_inc(sm["f_r"], 1)

            def final_stats(c, k):
                dve.wait_ge(sm["f_r"], c + 1)
                for q in range(QT):
                    dve.bn_stats(f_st6[:, k, q, :], r3[:, k, q, :]).then_inc(sm["f_st"], 1)

            def final_aggregate(c, k):
                wait(dve, sm["f_nmr"], c + 1 - FB)
                dve.wait_ge(sm["f_st"], QT * c + QT)
                for q in range(QT):
                    dve.bn_aggr(f_mv[:, k, q, :], f_st6[:, k, q, :]).then_inc(sm["f_mv"], 1)

            late_from = PARTS[0] + 1
            for c in range(NCH):
                final_sum(c, c % FB)
                if c > late_from:
                    final_aggregate(c - 1, (c - 1) % FB)
                final_stats(c, c % FB)
                if c < late_from or c == NCH - 1:
                    final_aggregate(c, c % FB)
            c, k = NCH - 1, (NCH - 1) % FB
            dve.wait_ge(sm["f_nmr"], NCH)
            for q in range(QT // 2, QT):
                ins = dve.tensor_scalar(res[:, c, q, :], r3[:, k, q, :], f_rstd[:, k, q:q + 1], f_nmr[:, k, q:q + 1], ALU.mult, ALU.add)
            ins.then_inc(sm["f_res_last"], 1)

        @block.tensor
        def _(pe):
            mm = pe.matmul
            pe.wait_ge(sm["const_ready"], 2)

            def x_transposed(c):
                pe.wait_ge(xr_loaded[c % 2], 16 * (c // 2 + 1))
                wait(pe, sm["xt_sb"], c)
                for q in range(QT):
                    last = pe.transpose(XT_PS[:, q * P:(q + 1) * P], xr[:, c % 2, q, :], ident[:])
                last.then_inc(sm["xT_ready"], 1)

            x_transposed(0)
            pe.wait_ge(sm["b_loaded"], 16 * 7)
            pe.wait_ge(sm["cc_ready"], 4)
            pe.transpose(Z_PS[:, 0:P], ball[:], ident[:])
            pe.transpose(Z_PS[:, P:2 * P], dm[:], ident[:])
            pe.transpose(Z_PS[:, 2 * P:3 * P], cc[:, 0, :], ident[:])
            pe.transpose(Z_PS[:, 3 * P:4 * P], cc[:, 1, :], ident[:]).then_inc(sm["setup_t"], 1)
            def products(out_, wh, wl, xh, xl, start, stop):
                mm(out_, wh, xh, start=start, stop=False)
                mm(out_, wh, xl, start=False, stop=False)
                return mm(out_, wl, xh, start=False, stop=stop)

            def inputs(c):
                pe.wait_ge(sm["x_lo"], c + 1)
                wait(pe, sm["p_ready"], c)
                products(BU_PS[:], bt_h[:], bt_l[:], xt_h[:, c % 2, :], xt_l[:, c % 2, :], True, True).then_inc(sm["bu_ready"], 1)

            def logits(c):
                pe.wait_ge(sm["r_ready"], c + 1)
                wait(pe, sm["lg_sb"], c)
                if c == PARTS[0] + 1:
                    pe.wait_ge(sm["rank_sb"], 1)
                for q in range(QT):
                    last = mm(LG_PS[:, q * E:(q + 1) * E], rt[:, q * P:(q + 1) * P], wgc[:], start=True, stop=True)
                last.then_inc(sm["lg_ready"], 1)

            def r_transposed(c):
                wait(pe, sm["row0_ready"], c)
                for q in range(QT):
                    last = pe.transpose(R_PS[:, q * D:(q + 1) * D], rt[:, q * P:(q + 1) * P], ident[:])
                last.then_inc(sm["rt_ready"], 1)

            def outputs(c):
                wait(pe, sm["y_lo"], c)
                pe.wait_ge(sm["q_ready"], 2 * c + 2)
                mm(Y_PS[:], wcs[:, 0, :], qc, start=True, stop=False)
                mm(Y_PS[:], wcs[:, 1, :], qs, start=False, stop=False)
                products(Y_PS[:], dt_h[:], dt_l[:], xt_h[:, c % 2, :], xt_l[:, c % 2, :], False, True).then_inc(sm["y_ready"], 1)

            def chunk(c):
                pe.wait_ge(sm["y_lo"], c + 1)
                for b in range(HB):
                    wait(pe, sm["h_act"], HB * c + b - 1)
                    products(H_PS[b % 2][:], w1_h[:, b * P:(b + 1) * P], w1_l[:, b * P:(b + 1) * P], y_h[:], y_l[:],
                             True, True).then_inc(sm["pre_a"], 1)
                    if b == 1:
                        if c + 2 < NCH:
                            x_transposed(c + 2)
                    if b == 2 and c >= 1:
                        logits(c - 1)
                if c + 1 < NCH:
                    outputs(c + 1)
                if c == PARTS[0] + 1:
                    pe.wait_ge(sm["lg_sb"], c)
                    ranks(0)
                wait(pe, sm["r_ready"], c)
                for b in range(HB):
                    if b == 2 and c + 2 < NCH:
                        inputs(c + 2)
                    if b == 3 and c >= 1:
                        r_transposed(c - 1)
                    pe.wait_ge(sm["hl_ready"], HB * c + b + 1)
                    products(Z_PS[:], w2_h[:, b * D:(b + 1) * D], w2_l[:, b * D:(b + 1) * D], h_h[:, b, :], h_l[:, b, :],
                             b == 0, b == HB - 1).then_inc(sm["z_ready"], 1)

            def ranks(p):
                pe.wait_ge(sm["const_ready"], 4)
                pe.wait_ge(sm["hits_ready"], p + 1)
                mm(LG_PS[:, 0:E], before[:], cnt[:, 0, :], start=True, stop=True)
                mm(LG_PS[:, E:2 * E], ones[:], cnt[:, 0, :], start=True, stop=True).then_inc(sm["rank_ready"], 1)

            x_transposed(1)
            pe.wait_ge(sm["setup_sb"], 1)
            inputs(0)
            pe.wait_ge(sm["ones_ready"], 1)
            pe.wait_ge(sm["bias_loaded"], 48)
            mm(LG_PS[:, 0:E], ones[:], wg[:], start=True, stop=True).then_inc(sm["wgm_ready"], 1)
            for b in range(HB + 1):
                last = pe.transpose(H_PS[0][:, b * E:(b + 1) * E], bst[:, b * P:(b + 1) * P], ident[0:E, 0:E])
            last.then_inc(sm["biasT_ready"], 1)
            outputs(0)
            inputs(1)
            pe.wait_ge(sm["w_ready"], 1)
            pe.wait_ge(sm["wgc_ready"], 1)
            pe.wait_ge(sm["fbias_ready"], 1)

            def xt(g, k):
                wait_loaded(pe, g, k)
                wait(pe, sm["xb_lo"], g)
                for q in range(SQ):
                    last = pe.transpose(XTB_PS[:, q * P:(q + 1) * P], xb[:, k, q, 0:D], ident[:])
                last.then_inc(sm["xTb_ready"], 1)

            def hidden(g, k, b):
                wait(pe, sm["gelu_b"], HB * g + (b - 1))
                products(H_PS[b % 2][:, 0:SLOTS], wuse[k][:, 0, b * P:(b + 1) * P], wuse[k][:, 1, b * P:(b + 1) * P],
                         xbt_h[k], xbt_l[k], True, True).then_inc(sm["preb_ready"], 1)

            def step(g, k, now, prev, nxt, far, nth):
                if now:
                    hidden(g, k, 2)
                    hidden(g, k, 3)
                if prev:
                    pe.wait_ge(sm["yt_ready"], g)
                    wait(pe, sm["yo_ready"], g - 2)
                    for q in range(SQ):
                        last = pe.transpose(YB_PS[1 - k][:, q * D:(q + 1) * D], yt[:, q * P:(q + 1) * P], ident[:])
                    last.then_inc(sm["yT_ready"], 1)
                if now:
                    pe.wait_ge(sm["w2use_ready"], g + 1)
                    for b in range(HB):
                        if b == 2 and nxt:
                            pe.wait_ge(sm["w1use_ready"], g + 2)
                            pe.wait_ge(sm["xb_lo"], g + 2)
                            hidden(g + 1, 1 - k, 0)
                            hidden(g + 1, 1 - k, 1)
                        if b == 3 and far:
                            xt(g + 2, k)
                        pe.wait_ge(sm["hbl_ready"], HB * g + (b + 1))
                        products(ZB_PS[k][:, 0:SLOTS], wuse[k][:, 2, b * D:(b + 1) * D], wuse[k][:, 3, b * D:(b + 1) * D],
                                 ht_h[b], ht_l[b], b == 0, b == HB - 1).then_inc(sm["zb_ready"], 1)


            for c in range(NCH):
                chunk(c)
            logits(NCH - 1)
            xt(0, 0)
            pe.wait_ge(sm["w1use_ready"], 1)
            pe.wait_ge(sm["xb_lo"], 1)
            hidden(0, 0, 0)
            hidden(0, 0, 1)
            xt(1, 1)
            r_transposed(NCH - 1)

            def after_last_rows():
                pe.wait_ge(sm["row0_ready"], NCH)
                ranks(1)

            walk(pe, MT, step, {ROUTE1 + 1: after_last_rows})

            def x1_sum(c):
                wait(pe, sm["f_r"], c + 1 - len(SUM_PS))
                out_ = SUM_PS[c % len(SUM_PS)][:, :].rearrange("p (q d) -> p q d", q=QT)
                mm(out_, ident[:], rows[:, 0, QT * c:QT * (c + 1), 0:D], start=True, stop=False)

            x1_before = {0: [0], 1: [1], 2: [2], 3: [3, 4, 5], 4: [6, 7]}
            for c in range(NCH):
                for n in x1_before.get(c, []):
                    x1_sum(n)
                pe.wait_ge(y0_loaded[c], 16)
                mm(SUM_PS[c % len(SUM_PS)][:], ident[:], y01(c)[:, 0], start=False, stop=True).then_inc(sm["f_sum"], 1)


def walk(eng, M, step, cuts):
    def one(g):
        if g in cuts:
            cuts[g]()
        step(g, g % 2, g < M, g >= 1, g + 1 < M, g + 2 < M, None)

    first = ROUTE1 + 3
    at = sorted({first, *(g for g in cuts if g > first), M - 2})
    for g in range(first):
        one(g)
    for a, b in zip(at, at[1:]):
        if a in cuts:
            cuts[a]()
        if b - a >= 2:
            with eng.Fori(0, (b - a) // 2) as i:
                for k in range(2):
                    step(2 * i + (a + k), (a + k) % 2, True, True, True, True, k)
        if (b - a) % 2:
            step(b - 1, (b - 1) % 2, True, True, True, True, None)
    one(M - 2)
    one(M - 1)
    one(M)


_INS = ["L0_attn_x3d", "L0_attn_nu_log", "L0_attn_theta_log", "L0_attn_B_re", "L0_attn_B_im", "L0_attn_C_re",
        "L0_attn_C_im", "L0_attn_D_mat", "L0_attn_W1", "L0_attn_W2", "L0_attn_res_logit",
        "L0_ffn_Wg", "L0_ffn_W1", "L0_ffn_b1", "L0_ffn_W2", "L0_ffn_b2"]
_OUTS = [((16, 256, 128), "float32")]


def kernel(**inputs):
    import numpy as _np
    import concourse.bacc as _bacc
    from concourse import mybir as _mybir
    from concourse.bass_utils import run_bass_kernel_spmd as _run

    nc = _bacc.Bacc("TRN2", target_bir_lowering=False, num_devices=1)
    arrays, args = {}, []
    for name in _INS:
        a = _np.ascontiguousarray(inputs[name])
        a = a.reshape(a.shape or (1,))
        arrays[f"in_{name}_dram"] = a
        args.append(nc.dram_tensor(f"in_{name}_dram", a.shape, _mybir.dt.from_np(a.dtype), kind="ExternalInput").ap())
    for i, (shape, dtype) in enumerate(_OUTS):
        dt = _mybir.dt.from_np(_np.dtype(dtype))
        args.append(nc.dram_tensor(f"out_{i}_dram", shape, dt, kind="ExternalOutput").ap())
    build(nc, *args)
    r = _run(nc, [arrays], core_ids=[0])
    return r.results[0]["out_0_dram"]
```
